# Optimizing a Trainium2 kernel written in Bass

```python
import numpy as np
import jax
import jax.numpy as jnp

def _softmax(x, axis=-1):
    return jax.nn.softmax(x, axis=axis)

def _gelu(x):
    return jax.nn.gelu(x, approximate=True)

def _silu(x):
    return jax.nn.silu(x)

def _sigmoid(x):
    return jax.nn.sigmoid(x)

def _layernorm(x, axis=-1, eps=1e-05):
    m = jnp.mean(x, axis=axis, keepdims=True)
    v = jnp.var(x, axis=axis, keepdims=True)
    return (x - m) / jnp.sqrt(v + eps)

def _scatter_add(tgt, idx, src, axis=0):
    return tgt.at[idx].add(src)

def _segment_sum(src, seg, n):
    return jax.ops.segment_sum(src, seg, n)
kernel_name = 'mk_seq_postln_d1_jaxref_r4_f63afd'

def setup_inputs(seed: int=0):
    np.random.seed(seed)
    _w = jnp.asarray

    def _L0_attn_setup():
        import jax, jax.numpy as jnp
        import numpy as np
        import math
        D = 512
        H = 16
        KV = 4
        DH = D // H
        REP = H // KV
        LAMBDA_INIT = 0.8 - 0.6 * math.exp(-0.3 * 0)
        ROPE_BASE = 10000.0
        EPS = 1e-05

        def _rope(x, cos, sin):
            x1, x2 = (x[..., ::2], x[..., 1::2])
            c = cos[None, None]
            s = sin[None, None]
            o1 = x1 * c - x2 * s
            o2 = x1 * s + x2 * c
            return jnp.stack([o1, o2], axis=-1).reshape(x.shape)

        def _forward(x, Wq, Wk, Wv, Wo, lambda_q1, lambda_k1, lambda_q2, lambda_k2, gn_w, gn_b):
            B, T, _ = x.shape
            q = (x @ Wq).reshape(B, T, H, 2 * DH).transpose(0, 2, 1, 3)
            k = (x @ Wk).reshape(B, T, KV, 2 * DH).transpose(0, 2, 1, 3)
            v = (x @ Wv).reshape(B, T, KV, 2 * DH).transpose(0, 2, 1, 3)
            q1, q2 = (q[..., :DH], q[..., DH:])
            k1, k2 = (k[..., :DH], k[..., DH:])
            inv = 1.0 / ROPE_BASE ** (jnp.arange(0, DH, 2, dtype=jnp.float32) / DH)
            freqs = jnp.arange(T, dtype=jnp.float32)[:, None] * inv[None, :]
            cos, sin = (jnp.cos(freqs), jnp.sin(freqs))
            q1, q2 = (_rope(q1, cos, sin), _rope(q2, cos, sin))
            k1, k2 = (_rope(k1, cos, sin), _rope(k2, cos, sin))
            k1 = jnp.repeat(k1, REP, axis=1)
            k2 = jnp.repeat(k2, REP, axis=1)
            v = jnp.repeat(v, REP, axis=1)
            mask = jnp.triu(jnp.full((T, T), -jnp.inf, dtype=x.dtype), k=1)[None, None]
            scale = 1.0 / math.sqrt(DH)
            s1 = jnp.einsum('bhtd,bhsd->bhts', q1, k1) * scale + mask
            s2 = jnp.einsum('bhtd,bhsd->bhts', q2, k2) * scale + mask
            a1 = jax.nn.softmax(s1, axis=-1)
            a2 = jax.nn.softmax(s2, axis=-1)
            lam = jnp.exp(jnp.sum(lambda_q1 * lambda_k1)) - jnp.exp(jnp.sum(lambda_q2 * lambda_k2)) + LAMBDA_INIT
            diff = a1 - lam * a2
            out = jnp.einsum('bhts,bhsd->bhtd', diff, v)
            out = out.transpose(0, 2, 1, 3)
            mean = jnp.mean(out, axis=(1, 3), keepdims=True)
            var = jnp.var(out, axis=(1, 3), keepdims=True)
            out = (out - mean) * jax.lax.rsqrt(var + EPS)
            out = out * gn_w.reshape(1, 1, H, 2 * DH) + gn_b.reshape(1, 1, H, 2 * DH)
            out = out.reshape(B, T, 2 * H * DH) * (1.0 - LAMBDA_INIT)
            return out @ Wo
        key = jax.random.key(seed)
        ks = jax.random.split(key, 12)
        B, T = (1, 512)
        s = 0.02
        return {'x': jax.random.normal(ks[0], (B, T, D), jnp.float32), 'Wq': jax.random.normal(ks[1], (D, 2 * H * DH), jnp.float32) * s, 'Wk': jax.random.normal(ks[2], (D, 2 * KV * DH), jnp.float32) * s, 'Wv': jax.random.normal(ks[3], (D, 2 * KV * DH), jnp.float32) * s, 'Wo': jax.random.normal(ks[4], (2 * H * DH, D), jnp.float32) * s, 'lambda_q1': jax.random.normal(ks[5], (DH,), jnp.float32) * 0.1, 'lambda_k1': jax.random.normal(ks[6], (DH,), jnp.float32) * 0.1, 'lambda_q2': jax.random.normal(ks[7], (DH,), jnp.float32) * 0.1, 'lambda_k2': jax.random.normal(ks[8], (DH,), jnp.float32) * 0.1, 'gn_w': jnp.ones((2 * H * DH,), jnp.float32), 'gn_b': jnp.zeros((2 * H * DH,), jnp.float32)}
    _L0_attn_in = _L0_attn_setup()

    def _L0_ffn_setup():
        import jax, jax.numpy as jnp
        import numpy as np
        B, S, H = (4, 512, 512)
        I = 352
        E = 8
        K = 2
        key = jax.random.key(seed)
        ks = jax.random.split(key, 5)
        sc_h = 1.0 / np.sqrt(H)
        sc_i = 1.0 / np.sqrt(I)
        return {'hidden_states': jax.random.normal(ks[0], (B, S, H), dtype=jnp.float32), 'gate_w': jax.random.normal(ks[1], (E, H), dtype=jnp.float32) * sc_h, 'w_gate': jax.random.normal(ks[2], (E, H, I), dtype=jnp.float32) * sc_h, 'w_up': jax.random.normal(ks[3], (E, H, I), dtype=jnp.float32) * sc_h, 'w_down': jax.random.normal(ks[4], (E, I, H), dtype=jnp.float32) * sc_i}
    _L0_ffn_in = _L0_ffn_setup()
    _d = {'L0_attn_x': _L0_attn_in['x'], 'L0_attn_Wq': _L0_attn_in['Wq'], 'L0_attn_Wk': _L0_attn_in['Wk'], 'L0_attn_Wv': _L0_attn_in['Wv'], 'L0_attn_Wo': _L0_attn_in['Wo'], 'L0_attn_lambda_q1': _L0_attn_in['lambda_q1'], 'L0_attn_lambda_k1': _L0_attn_in['lambda_k1'], 'L0_attn_lambda_q2': _L0_attn_in['lambda_q2'], 'L0_attn_lambda_k2': _L0_attn_in['lambda_k2'], 'L0_attn_gn_w': _L0_attn_in['gn_w'], 'L0_attn_gn_b': _L0_attn_in['gn_b'], 'L0_ffn_gate_w': _L0_ffn_in['gate_w'], 'L0_ffn_w_gate': _L0_ffn_in['w_gate'], 'L0_ffn_w_up': _L0_ffn_in['w_up'], 'L0_ffn_w_down': _L0_ffn_in['w_down']}
    _x0 = _d['L0_attn_x']
    _d['L0_attn_x'] = jax.random.normal(jax.random.fold_in(jax.random.key(seed), 1), (8, 512, 512), dtype=_x0.dtype)
    del _x0
    return _d

def reference(L0_attn_x, L0_attn_Wq, L0_attn_Wk, L0_attn_Wv, L0_attn_Wo, L0_attn_lambda_q1, L0_attn_lambda_k1, L0_attn_lambda_q2, L0_attn_lambda_k2, L0_attn_gn_w, L0_attn_gn_b, L0_ffn_gate_w, L0_ffn_w_gate, L0_ffn_w_up, L0_ffn_w_down):

    def _L0_attn_ref(x, Wq, Wk, Wv, Wo, lambda_q1, lambda_k1, lambda_q2, lambda_k2, gn_w, gn_b):
        import jax, jax.numpy as jnp
        import numpy as np
        import math
        D = 512
        H = 16
        KV = 4
        DH = D // H
        REP = H // KV
        LAMBDA_INIT = 0.8 - 0.6 * math.exp(-0.3 * 0)
        ROPE_BASE = 10000.0
        EPS = 1e-05

        def _rope(x, cos, sin):
            x1, x2 = (x[..., ::2], x[..., 1::2])
            c = cos[None, None]
            s = sin[None, None]
            o1 = x1 * c - x2 * s
            o2 = x1 * s + x2 * c
            return jnp.stack([o1, o2], axis=-1).reshape(x.shape)

        def _forward(x, Wq, Wk, Wv, Wo, lambda_q1, lambda_k1, lambda_q2, lambda_k2, gn_w, gn_b):
            B, T, _ = x.shape
            q = (x @ Wq).reshape(B, T, H, 2 * DH).transpose(0, 2, 1, 3)
            k = (x @ Wk).reshape(B, T, KV, 2 * DH).transpose(0, 2, 1, 3)
            v = (x @ Wv).reshape(B, T, KV, 2 * DH).transpose(0, 2, 1, 3)
            q1, q2 = (q[..., :DH], q[..., DH:])
            k1, k2 = (k[..., :DH], k[..., DH:])
            inv = 1.0 / ROPE_BASE ** (jnp.arange(0, DH, 2, dtype=jnp.float32) / DH)
            freqs = jnp.arange(T, dtype=jnp.float32)[:, None] * inv[None, :]
            cos, sin = (jnp.cos(freqs), jnp.sin(freqs))
            q1, q2 = (_rope(q1, cos, sin), _rope(q2, cos, sin))
            k1, k2 = (_rope(k1, cos, sin), _rope(k2, cos, sin))
            k1 = jnp.repeat(k1, REP, axis=1)
            k2 = jnp.repeat(k2, REP, axis=1)
            v = jnp.repeat(v, REP, axis=1)
            mask = jnp.triu(jnp.full((T, T), -jnp.inf, dtype=x.dtype), k=1)[None, None]
            scale = 1.0 / math.sqrt(DH)
            s1 = jnp.einsum('bhtd,bhsd->bhts', q1, k1) * scale + mask
            s2 = jnp.einsum('bhtd,bhsd->bhts', q2, k2) * scale + mask
            a1 = jax.nn.softmax(s1, axis=-1)
            a2 = jax.nn.softmax(s2, axis=-1)
            lam = jnp.exp(jnp.sum(lambda_q1 * lambda_k1)) - jnp.exp(jnp.sum(lambda_q2 * lambda_k2)) + LAMBDA_INIT
            diff = a1 - lam * a2
            out = jnp.einsum('bhts,bhsd->bhtd', diff, v)
            out = out.transpose(0, 2, 1, 3)
            mean = jnp.mean(out, axis=(1, 3), keepdims=True)
            var = jnp.var(out, axis=(1, 3), keepdims=True)
            out = (out - mean) * jax.lax.rsqrt(var + EPS)
            out = out * gn_w.reshape(1, 1, H, 2 * DH) + gn_b.reshape(1, 1, H, 2 * DH)
            out = out.reshape(B, T, 2 * H * DH) * (1.0 - LAMBDA_INIT)
            return out @ Wo
        return _forward(x, Wq, Wk, Wv, Wo, lambda_q1, lambda_k1, lambda_q2, lambda_k2, gn_w, gn_b)

    def _L0_ffn_ref(hidden_states, gate_w, w_gate, w_up, w_down):
        import jax, jax.numpy as jnp
        import numpy as np
        B, S, H = (4, 512, 512)
        I = 352
        E = 8
        K = 2
        b, s, h = hidden_states.shape
        x = hidden_states.reshape(-1, h)
        router_logits = x @ gate_w.T
        routing_weights = jax.nn.softmax(router_logits, axis=-1)
        topk_w, topk_i = jax.lax.top_k(routing_weights, K)
        topk_w = topk_w / jnp.sum(topk_w, axis=-1, keepdims=True)
        out = jnp.zeros_like(x)
        for e in range(w_gate.shape[0]):
            w_e = jnp.sum(jnp.where(topk_i == e, topk_w, 0.0), axis=-1)
            gated = jax.nn.silu(x @ w_gate[e]) * (x @ w_up[e])
            out = out + w_e[:, None] * (gated @ w_down[e])
        return out.reshape(b, s, h)
    x = L0_attn_x
    x = _layernorm(x + _L0_attn_ref(x, L0_attn_Wq, L0_attn_Wk, L0_attn_Wv, L0_attn_Wo, L0_attn_lambda_q1, L0_attn_lambda_k1, L0_attn_lambda_q2, L0_attn_lambda_k2, L0_attn_gn_w, L0_attn_gn_b), axis=-1)
    x = _layernorm(x + _L0_ffn_ref(x, L0_ffn_gate_w, L0_ffn_w_gate, L0_ffn_w_up, L0_ffn_w_down), axis=-1)
    return x

_drawn_inputs = setup_inputs


def setup_inputs(seed=0):
    import zlib

    import numpy as np

    out = dict(_drawn_inputs(seed))
    spreads = {'L0_attn_gn_w': (1.0, 0.2), 'L0_attn_gn_b': (0.0, 0.1)}
    factors = {'L0_attn_lambda_k1': 3.094, 'L0_attn_lambda_q2': 3.78, 'L0_attn_lambda_k2': 8.0}
    for name, (base, spread) in spreads.items():
        noise = np.random.default_rng([zlib.crc32(name.encode()), seed]).standard_normal(out[name].shape)
        drawn = base * np.exp(spread * noise) if base else spread * noise
        out[name] = jnp.asarray(drawn.astype(out[name].dtype))
    for name, factor in factors.items():
        out[name] = (out[name] * factor).astype(out[name].dtype)
    return out
```

```python
from contextlib import ExitStack
import math

import numpy as np

import concourse.bass as bass
from concourse import mybir

F32 = mybir.dt.float32
F32R = mybir.dt.float32r
BF16 = mybir.dt.bfloat16
I32 = mybir.dt.int32
U32 = mybir.dt.uint32
ALU = mybir.AluOpType
ACT = mybir.ActivationFunctionType
AX = mybir.AxisListType.X

P = 128
B, T, D = 8, 512, 512
H, KV, DH = 16, 4, 32
HD = 2 * DH
RK = H // KV
NT = T // P
DC = D // P
FC = H * HD // P
CQ = RK * HD + 2 * HD
NG = 2 * RK + 2
E, TOPK, I = 8, 2, 352
N = B * T
R = N + P
MT = (TOPK * N + E * (P - 1)) // P + 1
MT += MT % 2
EPS = 1e-5
LAMBDA_INIT = 0.8 - 0.6 * math.exp(-0.3 * 0)
NEG = -3.0e38

UNITS = [(0, (0, 1)), (0, (2, 3)), (1, (0, 1)), (1, (2, 3))] + [(i, (h,)) for i in (2, 3) for h in range(RK)]
NU = len(UNITS)
UB = NU * KV
assert UB % 6 == 0

LAG_T, LAG_V = 3, 4

PREP = {0: [("proj", 0)], 2: [("proj", 1)], 3: [("stack", 0)], 4: [("proj", 2)], 5: [("stack", 1)], 6: [("proj", 3)],
        7: [("stack", 2), ("stack", 3)], 8: [("stack", 4), ("stack", 5)], 9: [("stack", 6), ("stack", 7)],
        10: [("stack", 8)], 11: [("stack", 9)]}
PREP_ORDER = [x for s in sorted(PREP) for x in PREP[s]]
PREP_N = len(PREP_ORDER)
PREP_LEAD = 2 * NT + NG

TAIL_PE = {c + 3: [("ctxT", c)] for c in range(FC)}
TAIL_PE[13] = [("gn", 0)]
OP0 = 20
for _i in range(NT):
    for _q in range(4):
        TAIL_PE[OP0 + 4 * _i + _q] = [("oproj", _i, _q)]
TAIL_PE[OP0 + 20] = [("xT", 0)]
TAIL_PE[OP0 + 21] = [("xT", 1)]
TAIL_PE[OP0 + 22] = [("xT", 2)]
TAIL_PE[OP0 + 23] = [("xT", 3)]
TAIL_PE[OP0 + 24] = [("logits", 0)]
TAIL_PE[OP0 + 26] = [("rank", 0)]
TAIL_ORDER = [("ctxT", c) for c in range(FC)] + [("gn", 0)] + [("oproj", i) for i in range(NT)] \
    + [("xT", i) for i in range(NT)] + [("logits", 0), ("rank", 0)]
TAIL_N = len(TAIL_ORDER)


def layer_kernel(nc, x, xT_d, wqkv_d, wo_d, lam_d, gnw_d, gnb_d, gate_d, wg_d, wu_d, wd_d,
                 rope_cos_d, rope_sin_d, ident_d, identb_d, maskb_d, tri_d, avg_d, small_d, plan_d, out):
    x1_dram = nc.dram_tensor("x1_rows", [N, D], F32, kind="Internal").ap()
    xs_dram = nc.dram_tensor("expert_in_rows", [E * R, D], F32, kind="Internal").ap()
    ys_dram = nc.dram_tensor("expert_out_rows", [MT * P, D], F32, kind="Internal").ap()

    with ExitStack() as keep:
        def sbk(name, shape, dt=F32):
            return keep.enter_context(nc.sbuf_tensor(name, shape, dt))

        ident = sbk("ident", [P, P])
        ones = sbk("ones", [P, P])
        slots = sbk("slots", [P, N // P, TOPK], U32)
        wts = sbk("wts", [P, N // P, TOPK])
        msum = sbk("msum", [P, E])
        exp_tab = sbk("exp_tab", [1, MT], I32)
        row_tab = sbk("row_tab", [1, MT], I32)
        out_slots = sbk("out_slots", [P, N // P, TOPK], U32)
        attention_block(nc, x, xT_d, wqkv_d, wo_d, lam_d, gnw_d, gnb_d, gate_d, rope_cos_d, rope_sin_d,
                        ident_d, identb_d, maskb_d, tri_d, avg_d, small_d, x1_dram, xs_dram,
                        ident, ones, slots, wts, msum)
        plan_block(nc, plan_d, xs_dram, ones, msum, slots, out_slots, exp_tab, row_tab)
        expert_block(nc, wg_d, wu_d, wd_d, xs_dram, ys_dram, ident, exp_tab, row_tab)
        combine_block(nc, x1_dram, ys_dram, out_slots, wts, out)


def attention_block(nc, x, xT_d, wqkv_d, wo_d, lam_d, gnw_d, gnb_d, gate_d, rope_cos_d, rope_sin_d,
                    ident_d, identb_d, maskb_d, tri_d, avg_d, small_d, x1_dram, xs_dram,
                    ident, ones, slots, wts, msum):
    with ExitStack() as ctx:
        def sb(name, shape, dt=F32):
            return ctx.enter_context(nc.sbuf_tensor(name, shape, dt))

        def pb(name, shape, dt=F32):
            return ctx.enter_context(nc.psum_tensor(name, shape, dt))

        def sem(name):
            return ctx.enter_context(nc.semaphore(name))

        wqkv = sb("wqkv", [P, DC, KV, CQ])
        wo = sb("wo", [P, FC, D])
        gate = sb("gate", [P, DC, E])
        rcos = sb("rcos", [P, NT, NG, DH // 2])
        rsin = sb("rsin", [P, NT, NG, DH // 2])
        identb = sb("identb", [P, P], BF16)
        maskb = sb("maskb", [P, P], BF16)
        tri = sb("tri", [P, P])
        avg = sb("avg", [P, P])
        gnw = sb("gnw", [P, FC])
        gnb = sb("gnb", [P, FC])
        small = sb("small", [P, 2, NT, E])
        lam_in = sb("lam_in", [P, 4, DH])
        lam_pr = sb("lam_pr", [P, 2, DH])
        lam_s = sb("lam_s", [P, 2])
        lam_e = sb("lam_e", [P, 2])
        neg_lam = sb("neg_lam", [P, 1])
        eps_t = sb("eps_t", [P, 1])
        xT = sb("xT", [P, DC, T])
        qkv = sb("qkv", [P, NT, CQ])
        ra = sb("ra", [P, NT, NG, DH // 2])
        rb = sb("rb", [P, NT, NG, DH // 2])
        roped = sb("roped", [P, NT, NG, DH])
        split = sb("split", [P, NT * NG, P])
        qT = [sb(f"qT{r}", [P, 2 * RK, T], F32R) for r in range(2)]
        kT = [sb(f"kT{r}", [P, 2, T], F32R) for r in range(2)]
        vals = [sb(f"vals{r}", [P, NT, HD]) for r in range(KV)]
        neg_max = [sb(f"neg_max{r}", [P, 4]) for r in range(3)]
        sums = [sb(f"sums{r}", [P, NT, 2, RK]) for r in range(2)]
        rsum = [sb(f"rsum{r}", [P, NT, 2, RK]) for r in range(2)]
        rho = [sb(f"rho{r}", [P, NT, RK]) for r in range(2)]
        expd = [sb(f"expd{r}", [P, 1024]) for r in range(3)]
        mixed = [sb(f"mixed{r}", [P, 512]) for r in range(3)]
        probsT = [sb(f"probsT{r}", [P, 512]) for r in range(2)]
        ctxn = sb("ctxn", [P, NT, H * HD])
        ctxT = sb("ctxT", [P, FC, T])
        bn = sb("bn", [P, FC, 6])
        st = sb("st", [P, FC, 2])
        st2 = sb("st2", [P, FC, 2])
        gst = sb("gst", [P, FC, 2])
        gvar = sb("gvar", [P, FC])
        gsd = sb("gsd", [P, FC])
        grs = sb("grs", [P, FC])
        gsc = sb("gsc", [P, FC])
        gms = sb("gms", [P, FC])
        gbi = sb("gbi", [P, FC])
        x1 = sb("x1", [P, NT, D])
        bx = sb("bx", [P, NT, 6])
        mv = sb("mv", [P, NT, 2])
        xsd = sb("xsd", [P, NT])
        xrs = sb("xrs", [P, NT])
        lg = sb("lg", [P, NT, E])
        top = sb("top", [P, NT, E])
        topi = sb("topi", [P, NT, E], U32)
        topf = sb("topf", [P, NT, 2])
        pick = sb("pick", [P, 2, NT, E])
        member = sb("member", [P, NT, E])
        msum_t = sb("msum_t", [P, E])
        rank = sb("rank", [P, NT, E])
        pr = sb("pr", [P, 2, NT, E])
        slotf = sb("slotf", [P, TOPK, NT])
        dl = sb("dl", [P, NT])
        ed = sb("ed", [P, NT])
        ed1 = sb("ed1", [P, NT])

        S = [pb(f"S{r}", [P, 1024]) for r in range(2)]
        PTp = pb("PTp", [P, 512])
        O = pb("O", [P, RK, HD])
        prep = pb("prep", [P, 512])
        tail = pb("tail", [P, 512])

        consts_in = sem("consts_in")
        lam_step = sem("lam_step")
        lam_exp = sem("lam_exp")
        lam_ready = sem("lam_ready")
        xT_in = sem("xT_in")
        prep_full = sem("prep_full")
        prep_out = sem("prep_out")
        rope_step = sem("rope_step")
        rope_done = sem("rope_done")
        vals_ready = sem("vals_ready")
        hi_done = sem("hi_done")
        split_done = sem("split_done")
        scores_ready = sem("scores_ready")
        max_ready = sem("max_ready")
        exp_done = sem("exp_done")
        rsum_step = sem("rsum_step")
        rho_step = sem("rho_step")
        mix_ready = sem("mix_ready")
        pT_full = sem("pT_full")
        pT_out = sem("pT_out")
        ctx_full = sem("ctx_full")
        ctx_scaled = sem("ctx_scaled")
        tail_full = sem("tail_full")
        tail_act = sem("tail_act")
        tail_dve = sem("tail_dve")
        t_step = sem("t_step")
        gvar_ready = sem("gvar_ready")
        gsd_ready = sem("gsd_ready")
        norm_ready = sem("norm_ready")
        st_ready = sem("st_ready")
        x_in = sem("x_in")
        mv_ready = sem("mv_ready")
        xsd_ready = sem("xsd_ready")
        x1_ready = sem("x1_ready")
        member_ready = sem("member_ready")
        dl_ready = sem("dl_ready")
        ed_ready = sem("ed_ready")
        slots_ready = sem("slots_ready")
        x1_stored = sem("x1_stored")
        scattered = sem("scattered")
        NCONST = 14

        block = ctx.enter_context(nc.Block())

        waited = sem("waited")

        def apart(e):
            e.sem_inc(waited, 1)

        def at_least(e, s, v):
            if not isinstance(v, int) or v > 0:
                e.wait_ge(s, v)

        def prep_count(b, kv, kind, j, last=False):
            n = PREP_ORDER.index((kind, j))
            less = sum(k == "proj" for k, _ in PREP_ORDER[:n]) if last and kv == KV - 2 else 0
            return PREP_LEAD + PREP_N * (b * KV + kv) + n + 1 - less

        def tail_count(b, *task):
            return b * TAIL_N + TAIL_ORDER.index(task) + 1

        ACT_TAIL = [("ctxT", c) for c in range(FC)] + [("xT", i) for i in range(NT)]
        DVE_TAIL = [("gn", 0)] + [("oproj", i) for i in range(NT)] + [("logits", 0), ("rank", 0)]

        def tail_bank_free(e, b, *task):
            n = TAIL_ORDER.index(task)
            if n == 0:
                return
            before = TAIL_ORDER[n - 1]
            if before in ACT_TAIL:
                e.wait_ge(tail_act, b * len(ACT_TAIL) + ACT_TAIL.index(before) + 1)
            else:
                e.wait_ge(tail_dve, b * len(DVE_TAIL) + DVE_TAIL.index(before) + 1)

        def batches(eng, body, end):
            body(0, True, False)
            with eng.Fori(1, B - 1) as b:
                body(b, False, False)
            body(B - 1, False, True)
            end(B)

        def steps(b, first, last):
            for s in range(UB):
                yield s, s // NU, b * UB + s

        def lagged(b, s, lag, first):
            if first and s < lag:
                return None
            return (s - lag) % UB, b * UB + s - lag

        def preps(s, kv, last):
            for kind, j in PREP.get(s % NU, []):
                if last and (kv == KV - 1 or (kv == KV - 2 and kind == "proj")):
                    continue
                yield kind, j

        @block.sync
        def _(sp):
            for dst, src in ((xT[:], xT_d[:, 0]), (wqkv[:], wqkv_d), (ident[:], ident_d), (rcos[:], rope_cos_d),
                             (rsin[:], rope_sin_d), (lam_in[:], lam_d.unsqueeze(0).broadcast_to([P, 4, DH])),
                             (identb[:], identb_d), (maskb[:], maskb_d), (avg[:], avg_d), (tri[:], tri_d),
                             (gnw[:], gnw_d), (gnb[:], gnb_d), (small[:], small_d), (gate[:], gate_d),
                             (wo[:], wo_d)):
                first_one = src.name == xT_d.name
                sp.dma_start(dst, src).then_inc(xT_in if first_one else consts_in, 16)

            def load_x(b):
                sp.dma_start(x1[:], x[b].rearrange("(i p) d -> p i d", p=P)).then_inc(x_in, 16)

            def store_x1(b):
                sp.wait_ge(x1_ready, NT * (b + 1))
                sp.dma_start(x1_dram[bass.ds(b * T, T), :].rearrange("(i p) d -> p i d", p=P), x1[:]) \
                  .then_inc(x1_stored, 16)
                sp.wait_ge(x1_stored, 16 * (b + 1))
                apart(sp)
                sp.wait_ge(scattered, 16 * NT * TOPK * (b + 1))
                apart(sp)

            def body(b, first, last):
                if not first:
                    load_x(b - 1)
                if not last:
                    sp.wait_ge(prep_full, prep_count(b, 1, "proj", NT - 1))
                    sp.dma_start(xT[:], xT_d[:, b + 1]).then_inc(xT_in, 16)
                if not first:
                    store_x1(b - 1)

            def end(b):
                load_x(b - 1)
                store_x1(b - 1)

            batches(nc.sync, body, end)

        @block.gpsimd
        def _(pool):
            ROPE_OPS = 8

            def rope(n, kv, first_ever=False):
                pool.wait_ge(prep_out, proj_out(n))
                if not (isinstance(n, int) and n == 0):
                    pool.wait_ge(hi_done, n)
                xe = qkv[:, :, 0:NG * DH].rearrange("p t (g j two) -> p t g j two", g=NG, two=2)
                oe = roped[:].rearrange("p t g (j two) -> p t g j two", two=2)
                x0, x1_ = xe[:, :, :, :, 0], xe[:, :, :, :, 1]
                base = n * ROPE_OPS
                if not (isinstance(n, int) and n < KV):
                    pool.wait_ge(ctx_full, (n - KV + 1) * NU)
                apart(pool)
                nc.gpsimd.tensor_copy(vals[kv][:], qkv[:, :, NG * DH:CQ]).then_inc(vals_ready, 1)
                nc.gpsimd.tensor_tensor(ra[:], x0, rcos[:], ALU.mult).then_inc(rope_step, 1)
                nc.gpsimd.tensor_tensor(rb[:], x1_, rsin[:], ALU.mult).then_inc(rope_step, 1)
                pool.wait_ge(rope_step, base + 2)
                nc.gpsimd.tensor_tensor(oe[:, :, :, :, 0], ra[:], rb[:], ALU.subtract).then_inc(rope_step, 1)
                pool.wait_ge(rope_step, base + 3)
                nc.gpsimd.tensor_tensor(ra[:], x0, rsin[:], ALU.mult).then_inc(rope_step, 1)
                nc.gpsimd.tensor_tensor(rb[:], x1_, rcos[:], ALU.mult).then_inc(rope_step, 1)
                pool.wait_ge(rope_step, base + 5)
                nc.gpsimd.tensor_tensor(oe[:, :, :, :, 1], ra[:], rb[:], ALU.add).then_inc(rope_done, 1)
                pool.wait_ge(hi_done, n + 1)
                r2 = roped[:].rearrange("p t g d -> p (t g) d")
                nc.gpsimd.tensor_tensor(split[:, :, 3 * DH:4 * DH], r2, split[:, :, 0:DH], ALU.subtract) \
                  .then_inc(rope_step, 1)
                pool.wait_ge(rope_step, base + 6)
                apart(pool)
                s4 = split[:].rearrange("p (t g) f -> p t g f", g=NG)
                nc.gpsimd.tensor_copy(s4[:, :, 0:2 * RK, 2 * DH:3 * DH], s4[:, :, 0:2 * RK, 3 * DH:4 * DH]) \
                  .then_inc(rope_step, 1)
                nc.gpsimd.tensor_copy(s4[:, :, 2 * RK:NG, DH:2 * DH], s4[:, :, 2 * RK:NG, 3 * DH:4 * DH]) \
                  .then_inc(rope_step, 1)
                pool.wait_ge(rope_step, base + 8)
                nc.gpsimd.nop().then_inc(split_done, 1)

            def proj_out(n):
                if isinstance(n, int) and n < 2:
                    return NT * (n + 1)
                return PREP_LEAD + PREP_N * (n - 2) + PREP_ORDER.index(("proj", NT - 1)) + 1

            def scatter(b):
                for i in range(NT):
                    for k in range(TOPK):
                        nc.gpsimd.indirect_dma_start(
                            xs_dram, bass.IndirectOffsetOnAxis(ap=idx[:, i, k:k + 1], axis=0), x1[:, i, :], None,
                        ).then_inc(scattered, 16)

            idx = sb("idx", [P, NT, TOPK], U32)
            idx_copied = sem("idx_copied")

            def body(b, first, last):
                for kv in range(KV):
                    if not (last and kv >= KV - 2):
                        rope(b * KV + kv + 2, (kv + 2) % KV)
                if not first:
                    send(b - 1)

            def send(b):
                pool.wait_ge(slots_ready, b + 1)
                apart(pool)
                nc.gpsimd.tensor_copy(idx[:], slots[:, bass.ds(b * NT, NT), :]).then_inc(idx_copied, 1)
                pool.wait_ge(idx_copied, b + 1)
                pool.wait_ge(x1_ready, NT * (b + 1))
                apart(pool)
                scatter(b)

            def end(b):
                send(b - 1)
                pool.wait_ge(scattered, 16 * b * NT * TOPK)

            pool.wait_ge(consts_in, 16 * NCONST)
            rope(0, 0)
            rope(1, 1)
            batches(nc.gpsimd, body, end)

        @block.tensor
        def _(pe):
            def proj(n_kv, t, count):
                at_least(pe, prep_out, count - 1)
                for c in range(DC):
                    mm = nc.tensor.matmul(prep[:, 0:CQ], xT[:, c, t * P:(t + 1) * P], wqkv[:, c, n_kv, :],
                                          start=(c == 0), stop=(c == DC - 1))
                mm.then_inc(prep_full, 1)

            def stack(g, count):
                at_least(pe, prep_out, count - 1)
                for t in range(NT):
                    mm = nc.tensor.transpose(prep[:, t * P:(t + 1) * P], split[:, t * NG + g, :], ident[:])
                mm.then_inc(prep_full, 1)

            def scores(b, s, u, kv):
                i, heads = UNITS[s % NU]
                n = b * KV + kv
                if s % NU == 0:
                    pe.wait_ge(prep_out, stack_out(n))
                at_least(pe, exp_done, u - 1)
                slot, w = (256, 256) if i < 2 else (512, P * (i + 1))
                for a, h in enumerate(heads):
                    for c in range(2):
                        o = (2 * a + c) * slot
                        nc.tensor.matmul(S[s % 2][:, o:o + w], qT[kv % 2][:, 2 * h + c, i * P:(i + 1) * P],
                                         kT[kv % 2][:, c, 0:w], start=True, stop=False)
                        mm = nc.tensor.matmul(S[s % 2][:, o + i * P:o + (i + 1) * P], identb[:], maskb[:],
                                              start=False, stop=True)
                mm.then_inc(scores_ready, 1)

            def stack_out(n):
                if isinstance(n, int) and n == 0:
                    return PREP_LEAD
                less = NT if isinstance(n, int) and n == B * KV - 1 else 0
                return PREP_LEAD + PREP_N * (n - 1) + PREP_ORDER.index(("stack", NG - 1)) + 1 - less

            def transposes(sl, u):
                i, heads = UNITS[sl % NU]
                pe.wait_ge(mix_ready, u + 1)
                at_least(pe, pT_out, u)
                for a in range(len(heads)):
                    for j in range(i + 1):
                        o = (a * (i + 1) + j) * P
                        mm = nc.tensor.transpose(PTp[:, o:o + P], mixed[sl % 3][:, a * 256 + j * P:a * 256 + (j + 1) * P],
                                                 ident[:])
                mm.then_inc(pT_full, 1)

            def values(sl, u):
                i, heads = UNITS[sl % NU]
                kv = sl // NU
                pe.wait_ge(pT_out, u + 1)
                if heads[0] == 0:
                    at_least(pe, ctx_scaled, group_no(sl, u))
                for a, h in enumerate(heads):
                    for j in range(i + 1):
                        o = (a * (i + 1) + j) * P
                        mm = nc.tensor.matmul(O[:, h, :], probsT[sl % 2][:, o:o + P], vals[kv][:, j, :],
                                              start=(j == 0), stop=(j == i))
                mm.then_inc(ctx_full, 1)

            def group_no(sl, u):
                local = (sl // NU) * NT + UNITS[sl % NU][0]
                if isinstance(u, int):
                    return (u // UB) * KV * NT + local
                return batch_of(u, sl) * (KV * NT) + local

            batch_reg = [0]

            def batch_of(u, sl):
                return batch_reg[0] if sl < UB - LAG_V else batch_reg[0] - 1

            def tail_task(b, task):
                kind = task[0]
                if kind == "ctxT":
                    c = task[1]
                    if c % (FC // KV) == 0:
                        pe.wait_ge(ctx_scaled, (b * KV + c // (FC // KV) + 1) * NT)
                    tail_bank_free(pe, b, *task)
                    for i in range(NT):
                        mm = nc.tensor.transpose(tail[:, i * P:(i + 1) * P], ctxn[:, i, c * P:(c + 1) * P], ident[:])
                    mm.then_inc(tail_full, 1)
                elif kind == "gn":
                    pe.wait_ge(st_ready, b + 1)
                    tail_bank_free(pe, b, *task)
                    nc.tensor.matmul(tail[:, 0:2 * FC], avg[:], st2[:].rearrange("p c s -> p (c s)"),
                                     start=True, stop=True).then_inc(tail_full, 1)
                elif kind == "oproj":
                    i, q = task[1], task[2]
                    if q == 0:
                        pe.wait_ge(norm_ready, b + 1)
                        tail_bank_free(pe, b, "oproj", i)
                    for c in range(2 * q, 2 * q + 2):
                        mm = nc.tensor.matmul(tail[:], ctxT[:, c, i * P:(i + 1) * P], wo[:, c, :],
                                              start=(c == 0), stop=(c == FC - 1))
                    if q == 3:
                        mm.then_inc(tail_full, 1)
                elif kind == "xT":
                    i = task[1]
                    pe.wait_ge(x1_ready, b * NT + i + 1)
                    tail_bank_free(pe, b, *task)
                    for c in range(DC):
                        mm = nc.tensor.transpose(tail[:, c * P:(c + 1) * P], x1[:, i, c * P:(c + 1) * P], ident[:])
                    mm.then_inc(tail_full, 1)
                elif kind == "logits":
                    tail_bank_free(pe, b, *task)
                    for i in range(NT):
                        for c in range(DC):
                            mm = nc.tensor.matmul(tail[:, i * E:(i + 1) * E], ctxT[:, i, c * P:(c + 1) * P],
                                                  gate[:, c, :], start=(c == 0), stop=(c == DC - 1))
                    mm.then_inc(tail_full, 1)
                else:
                    pe.wait_ge(member_ready, b + 1)
                    tail_bank_free(pe, b, *task)
                    for i in range(NT):
                        o = tail[:, i * E:(i + 1) * E]
                        nc.tensor.matmul(o, ones[:], msum[:], start=True, stop=False)
                        for j in range(i):
                            nc.tensor.matmul(o, ones[:], member[:, j, :], start=False, stop=False)
                        mm = nc.tensor.matmul(o, tri[:], member[:, i, :], start=False, stop=True)
                    mm.then_inc(tail_full, 1)

            def body(b, first, last):
                batch_reg[0] = b
                for s, kv, u in steps(b, first, last):
                    scores(b, s, u, kv)
                    todo = list(preps(s, kv, last))

                    def prep_task():
                        if not todo:
                            return
                        kind, j = todo.pop(0)
                        count = prep_count(b, kv, kind, j, last)
                        if kind == "proj":
                            if j == 0 and kv == KV - 2:
                                pe.wait_ge(xT_in, 16 * (b + 2))
                            proj((kv + 2) % KV, j, count)
                        else:
                            if j == 0:
                                pe.wait_ge(split_done, b * KV + kv + 2)
                            stack(j, count)

                    prep_task()
                    if lagged(b, s, LAG_T, first):
                        transposes(*lagged(b, s, LAG_T, first))
                    prep_task()
                    if not first:
                        for task in TAIL_PE.get(s, []):
                            tail_task(b - 1, task)
                    if lagged(b, s, LAG_V, first):
                        values(*lagged(b, s, LAG_V, first))

            def end(b):
                batch_reg[0] = b
                for s in range(LAG_V):
                    if s < LAG_T:
                        transposes(*lagged(b, s, LAG_T, False))
                    values(*lagged(b, s, LAG_V, False))
                for s in sorted(TAIL_PE):
                    for task in TAIL_PE[s]:
                        tail_task(b - 1, task)

            pe.wait_ge(consts_in, 16 * NCONST)
            pe.wait_ge(xT_in, 16)
            for n in range(2):
                for t in range(NT):
                    proj(n, t, n * NT + t + 1)
            pe.wait_ge(split_done, 1)
            for g in range(NG):
                stack(g, 2 * NT + g + 1)
            pe.wait_ge(lam_ready, 1)
            batches(nc.tensor, body, end)

        @block.scalar
        def _(act):
            def take_proj(t, count, n):
                act.wait_ge(prep_full, count)
                if t == 0 and not (isinstance(n, int) and n == 0):
                    act.wait_ge(rope_done, n)
                nc.scalar.activation(qkv[:, t, :], prep[:, 0:CQ], ACT.Copy).then_inc(prep_out, 1)

            def take_stack(g, count, kvn):
                act.wait_ge(prep_full, count)
                dst = qT[kvn % 2][:, g, :] if g < 2 * RK else kT[kvn % 2][:, g - 2 * RK, :]
                nc.scalar.activation(dst, prep[:], ACT.Copy).then_inc(prep_out, 1)

            def exps(s, u):
                i, heads = UNITS[s % NU]
                kv = s // NU
                act.wait_ge(max_ready, u + 1)
                at_least(act, mix_ready, u - 2)
                slot, w = (256 if i < 2 else 512), P * (i + 1)
                for a, h in enumerate(heads):
                    for c in range(2):
                        k = 2 * a + c
                        ex = nc.scalar.activation(expd[s % 3][:, k * slot:k * slot + w], S[s % 2][:, k * slot:k * slot + w],
                                                  ACT.Exp, bias=neg_max[s % 3][:, k:k + 1], scale=1.0,
                                                  accum_out=sums[kv % 2][:, i, c, h:h + 1])
                ex.then_inc(exp_done, 1)

            def take_probsT(sl, u):
                i, heads = UNITS[sl % NU]
                w = len(heads) * (i + 1) * P
                act.wait_ge(pT_full, u + 1)
                at_least(act, ctx_full, u - 1)
                nc.scalar.activation(probsT[sl % 2][:, 0:w], PTp[:, 0:w], ACT.Copy).then_inc(pT_out, 1)

            def tail_task(b, task):
                kind = task[0]
                if kind == "ctxT":
                    c = task[1]
                    act.wait_ge(tail_full, tail_count(b, *task))
                    nc.scalar.activation(ctxT[:, c, :], tail[:], ACT.Copy).then_inc(tail_act, 1)
                elif kind == "xT":
                    act.wait_ge(tail_full, tail_count(b, *task))
                    nc.scalar.activation(ctxT[:, task[1], :], tail[:], ACT.Copy).then_inc(tail_act, 1)
                elif kind == "gn":
                    act.wait_ge(gvar_ready, b + 1)
                    nc.scalar.activation(gsd[:], gvar[:], ACT.Sqrt, bias=eps_t[:, 0:1]).then_inc(gsd_ready, 1)
                elif kind == "ln":
                    act.wait_ge(mv_ready, b + 1)
                    nc.scalar.activation(xsd[:], mv[:, :, 1], ACT.Sqrt, bias=eps_t[:, 0:1]).then_inc(xsd_ready, 1)
                elif kind == "wt":
                    act.wait_ge(dl_ready, b + 1)
                    nc.scalar.activation(ed[:], dl[:], ACT.Exp).then_inc(ed_ready, 1)

            mine = {s: list(v) for s, v in TAIL_PE.items()}
            mine[13] = []
            mine[14] = [("gn", 0)]
            mine[OP0 + 17] = [("ln", 0)]
            mine[OP0 + 26] = [("wt", 0)]

            def body(b, first, last):
                for s, kv, u in steps(b, first, last):
                    for kind, j in preps(s, kv, last):
                        count = prep_count(b, kv, kind, j, last)
                        if kind == "proj":
                            take_proj(j, count, b * KV + kv + 2)
                        else:
                            take_stack(j, count, kv + 1)
                    exps(s, u)
                    if lagged(b, s, LAG_T, first):
                        take_probsT(*lagged(b, s, LAG_T, first))
                    if not first:
                        for task in mine.get(s, []):
                            tail_task(b - 1, task)

            def end(b):
                for s in range(LAG_T):
                    take_probsT(*lagged(b, s, LAG_T, False))
                for s in sorted(mine):
                    for task in mine[s]:
                        tail_task(b - 1, task)

            act.wait_ge(lam_step, 3)
            nc.scalar.activation(lam_e[:], lam_s[:], ACT.Exp).then_inc(lam_exp, 1)
            for n in range(2):
                for t in range(NT):
                    take_proj(t, n * NT + t + 1, n)
            for g in range(NG):
                take_stack(g, 2 * NT + g + 1, 0)
            batches(nc.scalar, body, end)

        @block.vector
        def _(dve):
            def high_parts(n):
                dve.wait_ge(rope_done, n + 1)
                if not (isinstance(n, int) and n == 0):
                    dve.wait_ge(prep_full, stack_read(n - 1))
                r2 = roped[:].rearrange("p t g d -> p (t g) d")
                s4 = split[:].rearrange("p (t g) f -> p t g f", g=NG)
                nc.vector.tensor_copy(split[:, :, 0:DH].bitcast(F32R), r2)
                nc.vector.tensor_copy(s4[:, :, 0:2 * RK, DH:2 * DH].bitcast(F32R), roped[:, :, 0:2 * RK, :])
                nc.vector.tensor_copy(s4[:, :, 2 * RK:NG, 2 * DH:3 * DH].bitcast(F32R),
                                      roped[:, :, 2 * RK:NG, :]).then_inc(hi_done, 1)

            def stack_read(n):
                if isinstance(n, int) and n == 0:
                    return PREP_LEAD
                return PREP_LEAD + PREP_N * (n - 1) + PREP_ORDER.index(("stack", NG - 1)) + 1

            def maxes(s, u):
                i, heads = UNITS[s % NU]
                dve.wait_ge(scores_ready, u + 1)
                slot, w, k = (256 if i < 2 else 512), P * (i + 1), 2 * len(heads)
                v = S[s % 2][:, 0:k * slot].rearrange("p (k w) -> p k w", w=slot)[:, :, 0:w]
                nc.vector.tensor_reduce(neg_max[s % 3][:, 0:k], v, AX, ALU.max, negate=True).then_inc(max_ready, 1)

            def inverse_sums(sl, u):
                i, heads = UNITS[sl % NU]
                kv = sl // NU
                h0, nh = heads[0], len(heads)
                dve.wait_ge(exp_done, u + 1)
                L, Q = sums[kv % 2], rsum[kv % 2]
                nc.vector.reciprocal(Q[:, i, :, h0:h0 + nh], L[:, i, :, h0:h0 + nh]).then_inc(rsum_step, 1)

            def ratios(sl, u):
                i, heads = UNITS[sl % NU]
                kv = sl // NU
                h0, nh = heads[0], len(heads)
                L, Q, rr = sums[kv % 2], rsum[kv % 2], rho[kv % 2]
                dve.wait_ge(rsum_step, u + 1)
                nc.vector.scalar_tensor_tensor(out=rr[:, i, h0:h0 + nh], in0=L[:, i, 0, h0:h0 + nh],
                                               scalar=neg_lam[:, 0:1], in1=Q[:, i, 1, h0:h0 + nh],
                                               op0=ALU.mult, op1=ALU.mult).then_inc(rho_step, 1)

            def mix(sl, u):
                i, heads = UNITS[sl % NU]
                rr = rho[sl // NU % 2]
                slot, w = (256 if i < 2 else 512), P * (i + 1)
                dve.wait_ge(rho_step, u + 1)
                at_least(dve, pT_full, u - 2)
                for a, h in enumerate(heads):
                    e1 = expd[sl % 3][:, 2 * a * slot:2 * a * slot + w]
                    e2 = expd[sl % 3][:, (2 * a + 1) * slot:(2 * a + 1) * slot + w]
                    ins = nc.vector.scalar_tensor_tensor(out=mixed[sl % 3][:, a * 256:a * 256 + w], in0=e2,
                                                         scalar=rr[:, i, h:h + 1], in1=e1, op0=ALU.mult, op1=ALU.add)
                ins.then_inc(mix_ready, 1)

            def scale_out(b, sl, u):
                i, heads = UNITS[sl % NU]
                kv = sl // NU
                if heads[-1] != RK - 1:
                    return
                dve.wait_ge(ctx_full, u + 1)
                if i == 0 and not (isinstance(b, int) and b == 0):
                    dve.wait_ge(tail_full, tail_count(b - 1, "ctxT", (kv + 1) * (FC // KV) - 1))
                nc.vector.tensor_tensor(ctxn[:, i, kv * RK * HD:(kv + 1) * RK * HD].rearrange("p (h d) -> p h d", h=RK),
                                        O[:], rsum[kv % 2][:, i, 0, :].unsqueeze(2).broadcast_to([P, RK, HD]),
                                        ALU.mult).then_inc(ctx_scaled, 1)

            links = [0]
            LINKS = 21

            def link(b, ins):
                links[0] += 1
                ins.then_inc(t_step, 1)
                dve.wait_ge(t_step, b * LINKS + links[0])

            def tail_work(b, what, j):
                if what == "bn":
                    dve.wait_ge(tail_act, b * len(ACT_TAIL) + j + 1)
                    ins = nc.vector.bn_stats(out=bn[:, j, :], in_=ctxT[:, j, :])
                    if j == FC - 1:
                        link(b, ins)
                        apart(dve)
                elif what == "gstats":
                    for c in range(FC):
                        ins = nc.vector.bn_aggr(st[:, c, :], bn[:, c, :])
                    link(b, ins)
                    nc.vector.tensor_copy(st2[:, :, 0], st[:, :, 0])
                    link(b, nc.vector.tensor_tensor(st2[:, :, 1], st[:, :, 0], st[:, :, 0], ALU.mult))
                    nc.vector.tensor_tensor(st2[:, :, 1], st2[:, :, 1], st[:, :, 1], ALU.add).then_inc(st_ready, 1)
                elif what == "gvar":
                    dve.wait_ge(tail_full, tail_count(b, "gn", 0))
                    ins = nc.vector.tensor_copy(gst[:].rearrange("p c s -> p (c s)"), tail[:, 0:2 * FC])
                    ins.then_inc(tail_dve, 1)
                    dve.wait_ge(tail_dve, b * len(DVE_TAIL) + 1)
                    link(b, nc.vector.tensor_tensor(gvar[:], gst[:, :, 0], gst[:, :, 0], ALU.mult))
                    nc.vector.tensor_tensor(gvar[:], gst[:, :, 1], gvar[:], ALU.subtract).then_inc(gvar_ready, 1)
                elif what == "gaffine":
                    dve.wait_ge(gsd_ready, b + 1)
                    link(b, nc.vector.reciprocal(grs[:], gsd[:]))
                    link(b, nc.vector.scalar_tensor_tensor(out=gsc[:], in0=grs[:], scalar=1.0 - LAMBDA_INIT, in1=gnw[:],
                                                           op0=ALU.mult, op1=ALU.mult))
                    link(b, nc.vector.tensor_tensor(gms[:], gst[:, :, 0], gsc[:], ALU.mult))
                    link(b, nc.vector.scalar_tensor_tensor(out=gbi[:], in0=gnb[:], scalar=1.0 - LAMBDA_INIT, in1=gms[:],
                                                           op0=ALU.mult, op1=ALU.subtract))
                elif what == "norm":
                    ins = nc.vector.tensor_scalar(ctxT[:, j, :], ctxT[:, j, :], gsc[:, j:j + 1], gbi[:, j:j + 1],
                                                  ALU.mult, ALU.add)
                    if j == FC - 1:
                        ins.then_inc(norm_ready, 1)
                elif what == "resid":
                    if j == 0:
                        dve.wait_ge(x_in, 16 * (b + 1))
                    dve.wait_ge(tail_full, tail_count(b, "oproj", j))
                    nc.vector.tensor_tensor(x1[:, j, :], tail[:], x1[:, j, :], ALU.add).then_inc(tail_dve, 1)
                    dve.wait_ge(tail_dve, b * len(DVE_TAIL) + DVE_TAIL.index(("oproj", j)) + 1)
                    link(b, nc.vector.bn_stats(out=bx[:, j, :], in_=x1[:, j, :]))
                    apart(dve)
                    ins = nc.vector.bn_aggr(mv[:, j, :], bx[:, j, :])
                    if j == NT - 1:
                        ins.then_inc(mv_ready, 1)
                elif what == "ln":
                    if j == 0:
                        dve.wait_ge(xsd_ready, b + 1)
                        link(b, nc.vector.reciprocal(xrs[:], xsd[:]))
                    nc.vector.tensor_scalar(x1[:, j, :], x1[:, j, :], mv[:, j, 0:1], xrs[:, j:j + 1],
                                            ALU.subtract, ALU.mult).then_inc(x1_ready, 1)
                elif what == "route":
                    dve.wait_ge(tail_full, tail_count(b, "logits", 0))
                    nc.vector.tensor_copy(lg[:].rearrange("p i e -> p (i e)"), tail[:, 0:NT * E]).then_inc(tail_dve, 1)
                    dve.wait_ge(tail_dve, b * len(DVE_TAIL) + DVE_TAIL.index(("logits", 0)) + 1)
                    apart(dve)
                    for i in range(NT):
                        ins = nc.vector.max(top[:, i, :], lg[:, i, :])
                    link(b, ins)
                    apart(dve)
                    for i in range(NT):
                        ins = nc.vector.max_index(topi[:, i, :], top[:, i, :], lg[:, i, :])
                    link(b, ins)
                    nc.vector.tensor_tensor(dl[:], top[:, :, 1], top[:, :, 0], ALU.subtract).then_inc(dl_ready, 1)
                    link(b, nc.vector.tensor_copy(topf[:], topi[:, :, 0:2]))
                    for k in range(TOPK):
                        ins = nc.vector.tensor_tensor(pick[:, k], small[:, 0], topf[:, :, k:k + 1].broadcast_to([P, NT, E]),
                                                      ALU.is_equal)
                    link(b, ins)
                    nc.vector.tensor_tensor(member[:], pick[:, 0], pick[:, 1], ALU.add).then_inc(member_ready, 1)
                elif what == "slots":
                    dve.wait_ge(tail_full, tail_count(b, "rank", 0))
                    nc.vector.tensor_tensor(rank[:].rearrange("p i e -> p (i e)"), tail[:, 0:NT * E],
                                            small[:, 1].rearrange("p i e -> p (i e)"), ALU.add).then_inc(tail_dve, 1)
                    dve.wait_ge(tail_dve, b * len(DVE_TAIL) + DVE_TAIL.index(("rank", 0)) + 1)
                    for k in range(TOPK):
                        nc.vector.tensor_tensor(pr[:, k], rank[:], pick[:, k], ALU.mult)
                    link(b, nc.vector.tensor_reduce(msum_t[:], member[:].rearrange("p i e -> p e i"), AX, ALU.add))
                    nc.vector.tensor_tensor(msum[:], msum[:], msum_t[:], ALU.add)
                    here = bass.ds(b * NT, NT)
                    link(b, nc.vector.tensor_reduce(slotf[:].rearrange("p k i -> p (k i)"),
                                                    pr[:].rearrange("p k i e -> p (k i) e"), AX, ALU.add))
                    nc.vector.tensor_copy(slots[:, here, :], slotf[:].rearrange("p k i -> p i k")).then_inc(slots_ready, 1)
                    dve.wait_ge(ed_ready, b + 1)
                    link(b, nc.vector.tensor_scalar(ed1[:], ed[:], 1.0, None, ALU.add))
                    link(b, nc.vector.reciprocal(wts[:, here, 0], ed1[:]))
                    nc.vector.tensor_tensor(wts[:, here, 1], ed[:], wts[:, here, 0], ALU.mult)

            mine = {c + 4: [("bn", c)] for c in range(FC)}
            mine[11] = mine.get(11, []) + [("gstats", 0)]
            mine[14] = [("gvar", 0)]
            mine[15] = [("gaffine", 0), ("norm", 0)]
            for c in range(1, FC):
                mine.setdefault(15 + c // 2 + c % 2, []).append(("norm", c))
            for i in range(NT):
                mine.setdefault(OP0 + 4 * i + 4, []).append(("resid", i))
            for i in range(NT):
                mine.setdefault(OP0 + 18 + i // 2, []).append(("ln", i))
            mine[OP0 + 25] = [("route", 0)]
            mine[OP0 + 27] = [("slots", 0)]

            def body(b, first, last):
                links[0] = 0
                for s, kv, u in steps(b, first, last):
                    if lagged(b, s, LAG_V + 1, first):
                        scale_out(b if s > LAG_V else b - 1, *lagged(b, s, LAG_V + 1, first))
                    maxes(s, u)
                    if lagged(b, s, 1, first):
                        inverse_sums(*lagged(b, s, 1, first))
                    if lagged(b, s, 2, first):
                        mix(*lagged(b, s, 2, first))
                    if lagged(b, s, 1, first):
                        ratios(*lagged(b, s, 1, first))
                    if s % NU == HI_STEP and not (last and kv >= KV - 2):
                        high_parts(b * KV + kv + 2 - HI_LAG)
                    if s % NU == HI_STEP and last and kv >= KV - 2 and kv - (KV - 2) < HI_LAG:
                        high_parts(b * KV + kv + 2 - HI_LAG)
                    if not first:
                        for what, j in mine.get(s, []):
                            tail_work(b - 1, what, j)

            def end(b):
                links[0] = 0
                inverse_sums(*lagged(b, 0, 1, False))
                mix(*lagged(b, 0, 2, False))
                ratios(*lagged(b, 0, 1, False))
                mix(*lagged(b, 1, 2, False))
                for s in range(LAG_V + 1):
                    scale_out(b - 1, *lagged(b, s, LAG_V + 1, False))
                for s in sorted(mine):
                    for what, j in mine[s]:
                        tail_work(b - 1, what, j)
                assert links[0] == LINKS, links[0]

            nc.vector.memset(ones[:], 1.0)
            nc.vector.memset(msum[:], 0.0)
            nc.vector.memset(eps_t[:], EPS).then_inc(lam_step, 1)
            dve.wait_ge(consts_in, 16 * NCONST)
            lv = lam_in[:].rearrange("p (c two) d -> p c two d", two=2)
            nc.vector.tensor_tensor(lam_pr[:], lv[:, :, 0], lv[:, :, 1], ALU.mult).then_inc(lam_step, 1)
            dve.wait_ge(lam_step, 2)
            nc.vector.tensor_reduce(lam_s[:], lam_pr[:], AX, ALU.add).then_inc(lam_step, 1)
            dve.wait_ge(lam_exp, 1)
            nc.vector.scalar_tensor_tensor(out=neg_lam[:], in0=lam_e[:, 1:2], scalar=-LAMBDA_INIT, in1=lam_e[:, 0:1],
                                           op0=ALU.add, op1=ALU.subtract).then_inc(lam_ready, 1)
            dve.wait_ge(lam_ready, 1)
            high_parts(0)
            if HI_LAG == 0:
                high_parts(1)
            batches(nc.vector, body, end)


HI_STEP = 0
HI_LAG = 1


def plan_block(nc, plan_d, xs_dram, ones, msum, slots, out_slots, exp_tab, row_tab):
    with ExitStack() as ctx:
        def sb(name, shape, dt=F32):
            return ctx.enter_context(nc.sbuf_tensor(name, shape, dt))

        def sem(name):
            return ctx.enter_context(nc.semaphore(name))

        plan = sb("plan", [P, 2 * E + E * E + 2 * MT * E])
        zrow = sb("zrow", [P, D])
        cnt = sb("cnt", [P, E])
        padf = sb("padf", [P, E])
        padi = sb("padi", [P, E], U32)
        ni = sb("ni", [P, E], I32)
        ni2 = sb("ni2", [P, E], I32)
        nt = sb("nt", [P, E])
        gap = sb("gap", [P, E])
        sf = sb("sf", [P, N // P * TOPK])
        so = sb("so", [P, N // P * TOPK])
        hop = sb("hop", [P, E - 1, N // P * TOPK])
        cp = sb("cp", [1, E, E])
        ci = sb("ci", [1, E])
        ge = sb("ge", [1, MT, E])
        gn = sb("gn", [1, MT, E])
        ek = sb("ek", [1, MT])
        sk = sb("sk", [1, MT])
        live = sb("live", [1, MT])
        jk = sb("jk", [1, MT])
        rk = sb("rk", [1, MT])
        cps = ctx.enter_context(nc.psum_tensor("cps", [P, E], F32))
        plan_in = sem("plan_in")
        cnt_full = sem("cnt_full")
        chain = sem("chain")
        pad_ready = sem("pad_ready")
        padded = sem("padded")
        block = ctx.enter_context(nc.Block())
        region = plan[:, 0:E]
        incl = plan[0:1, 2 * E:2 * E + E * E].rearrange("p (a b) -> p a b", a=E)
        kio = plan[0:1, 2 * E + E * E:2 * E + E * E + MT * E].rearrange("p (k e) -> p k e", e=E)

        @block.sync
        def _(sp):
            sp.dma_start(plan[:], plan_d).then_inc(plan_in, 16)

        @block.tensor
        def _(pe):
            nc.tensor.matmul(cps[:], ones[:], msum[:], start=True, stop=True).then_inc(cnt_full, 1)

        @block.gpsimd
        def _(pool):
            pool.wait_ge(pad_ready, 1)
            for e in range(E):
                nc.gpsimd.indirect_dma_start(xs_dram, bass.IndirectOffsetOnAxis(ap=padi[:, e:e + 1], axis=0),
                                             zrow[:], None).then_inc(padded, 16)
            pool.wait_ge(padded, 16 * E)

        @block.vector
        def _(dve):
            links = [0]

            def link(ins):
                links[0] += 1
                ins.then_inc(chain, 1)
                dve.wait_ge(chain, links[0])

            nc.vector.memset(zrow[:], 0.0)
            dve.wait_ge(plan_in, 16)
            dve.wait_ge(cnt_full, 1)
            link(nc.vector.tensor_copy(cnt[:], cps[:]))
            link(nc.vector.tensor_tensor(padf[:], cnt[:], region, ALU.add))
            nc.vector.tensor_copy(padi[:], padf[:]).then_inc(pad_ready, 1)
            link(nc.vector.tensor_scalar(nt[:], cnt[:], float(P - 1), None, ALU.add))
            link(nc.vector.tensor_copy(ni[:], nt[:]))
            link(nc.vector.tensor_scalar(ni2[:], ni[:], P.bit_length() - 1, None, ALU.arith_shift_right))
            link(nc.vector.tensor_copy(nt[:], ni2[:]))
            nc.vector.tensor_copy(sf[:], slots[:].rearrange("p t k -> p (t k)"))
            link(nc.vector.tensor_scalar(gap[:], nt[:], float(P), -float(R), ALU.mult, ALU.add))
            for e in range(1, E):
                ins = nc.vector.tensor_scalar(hop[:, e - 1, :], sf[:], float(e * R), gap[:, e - 1:e], ALU.is_ge, ALU.mult)
            link(ins)
            link(nc.vector.tensor_reduce(so[:], hop[:].rearrange("p e s -> p s e"), AX, ALU.add))
            link(nc.vector.tensor_tensor(so[:], so[:], sf[:], ALU.add))
            nc.vector.tensor_copy(out_slots[:].rearrange("p t k -> p (t k)"), so[:])
            link(nc.vector.tensor_tensor(cp[:], incl, nt[0:1, :].unsqueeze(1).broadcast_to([1, E, E]), ALU.mult))
            link(nc.vector.tensor_reduce(ci[:], cp[:], AX, ALU.add))
            link(nc.vector.tensor_tensor(ge[:], kio, ci[:].unsqueeze(1).broadcast_to([1, MT, E]), ALU.is_ge))
            link(nc.vector.tensor_tensor(gn[:], ge[:], nt[0:1, :].unsqueeze(1).broadcast_to([1, MT, E]), ALU.mult))
            nc.vector.tensor_reduce(ek[:], ge[:], AX, ALU.add)
            link(nc.vector.tensor_reduce(sk[:], gn[:], AX, ALU.add))
            link(nc.vector.tensor_scalar(live[:], ge[:, :, E - 1], -1.0, 1.0, ALU.mult, ALU.add))
            link(nc.vector.tensor_tensor(jk[:], kio[:, :, 0], sk[:], ALU.subtract))
            link(nc.vector.tensor_tensor(jk[:], jk[:], live[:], ALU.mult))
            link(nc.vector.tensor_tensor(ek[:], ek[:], live[:], ALU.mult))
            link(nc.vector.tensor_scalar(rk[:], ek[:], float(R), None, ALU.mult))
            link(nc.vector.scalar_tensor_tensor(out=rk[:], in0=jk[:], scalar=float(P), in1=rk[:],
                                                op0=ALU.mult, op1=ALU.add))
            nc.vector.tensor_copy(exp_tab[:], ek[:])
            link(nc.vector.tensor_copy(row_tab[:], rk[:]))


def expert_block(nc, wg_d, wu_d, wd_d, xs_dram, ys_dram, ident, exp_tab, row_tab):
    IC = [(0, P), (P, P), (2 * P, I - 2 * P)]
    with ExitStack() as ctx:
        def sb(name, shape, dt=F32):
            return ctx.enter_context(nc.sbuf_tensor(name, shape, dt))

        def pb(name, shape):
            return ctx.enter_context(nc.psum_tensor(name, shape, F32))

        def sem(name):
            return ctx.enter_context(nc.semaphore(name))

        GU = 2 * I
        wgu = sb("wgu", [P, E * DC * GU])
        wgu_v = wgu[:].rearrange("p (e c g i) -> p e c g i", e=E, c=DC, g=2)
        wd = sb("wd", [P, E * len(IC) * D])
        wd_v = wd[:].rearrange("p (e c d) -> p e c d", e=E, c=len(IC))
        xin = [sb(f"xin{r}", [P, D]) for r in range(2)]
        xinT = [sb(f"xinT{r}", [P, D]) for r in range(2)]
        sg = [sb(f"sg{r}", [P, I]) for r in range(2)]
        hid = [sb(f"hid{r}", [P, I]) for r in range(2)]
        hidT = [sb(f"hidT{r}", [P, 3 * P]) for r in range(2)]
        yo = [sb(f"yo{r}", [P, D]) for r in range(2)]
        xTp = pb("xTp", [P, 512])
        G = [pb(f"G{r}", [P, 512]) for r in range(2)]
        U = [pb(f"U{r}", [P, 512]) for r in range(2)]
        hTp = pb("hTp", [P, 512])
        Y = [pb(f"Y{r}", [P, 512]) for r in range(2)]

        w_in = sem("w_in")
        rows_in = [sem(f"rows_in{r}") for r in range(2)]
        xT_full = sem("e_xT_full")
        xT_out = sem("e_xT_out")
        g_full = sem("g_full")
        gu_full = sem("gu_full")
        silu_done = sem("silu_done")
        hid_ready = sem("hid_ready")
        hT_full = sem("hT_full")
        hT_out = sem("hT_out")
        y_full = sem("y_full")
        y_out = sem("y_out")
        y_stored = [sem(f"y_stored{r}") for r in range(2)]
        block = ctx.enter_context(nc.Block())
        NW = 4 * E

        def load_weights(eng, experts):
            for e in experts:
                eng.dma_start(wgu_v[:, e, :, 0, :], wg_d[e].rearrange("(c p) i -> p c i", p=P)).then_inc(w_in, 16)
                eng.dma_start(wgu_v[:, e, :, 1, :], wu_d[e].rearrange("(c p) i -> p c i", p=P)).then_inc(w_in, 16)
                eng.dma_start(wd_v[:, e, 0:2, :], wd_d[e, 0:2 * P].rearrange("(c p) d -> p c d", p=P)).then_inc(w_in, 16)
                eng.dma_start(wd_v[0:I - 2 * P, e, 2, :], wd_d[e, 2 * P:I]).then_inc(w_in, 16)

        @block.sync
        def _(sp):
            def load(k, r, wait):
                row = nc.sync.value_load(row_tab[0:1, bass.ds(k, 1)], min_val=0, max_val=(E - 1) * R + N)
                if wait:
                    sp.wait_ge(xT_full, k - 1)
                sp.dma_start(xin[r][:], xs_dram[bass.ds(row, P), :]).then_inc(rows_in[r], 16)

            load(0, 0, False)
            load(1, 1, False)
            load_weights(sp, range(0, E, 2))
            with nc.sync.Fori(1, MT // 2) as m:
                for r in range(2):
                    load(m * 2 + r, r, True)

        @block.scalar
        def _(act):
            load_weights(act, range(1, E, 2))

            def take_xT(k, r):
                act.wait_ge(xT_full, k + 1)
                if not (isinstance(k, int) and k < 2):
                    act.wait_ge(gu_full, k - 1)
                nc.scalar.activation(xinT[r][:], xTp[:], ACT.Copy).then_inc(xT_out, 1)

            def silu(k, r):
                act.wait_ge(g_full, k + 1)
                if not (isinstance(k, int) and k < 2):
                    act.wait_ge(hid_ready, k - 1)
                nc.scalar.activation(sg[r][:], G[r][:, 0:I], ACT.Silu).then_inc(silu_done, 1)

            def store(k, r):
                act.wait_ge(y_out, k + 1)
                act.dma_start(ys_dram[bass.ds(k * P, P), :], yo[r][:]).then_inc(y_stored[r], 16)

            take_xT(0, 0)
            take_xT(1, 1)
            silu(0, 0)

            def pair(m):
                for r in range(2):
                    k = m * 2 + r
                    take_xT(k + 2, r)
                    silu(k + 1, 1 - r)
                    store(k, r)

            pair(0)
            with nc.scalar.Fori(1, MT // 2 - 1) as m:
                pair(m)
            silu(MT - 1, 1)
            store(MT - 2, 0)
            store(MT - 1, 1)
            for r in range(2):
                act.wait_ge(y_stored[r], 16 * MT // 2)

        @block.tensor
        def _(pe):
            def expert(k):
                return nc.tensor.value_load(exp_tab[0:1, bass.ds(k, 1)], min_val=0, max_val=E - 1)

            def x_transpose(k, r):
                pe.wait_ge(rows_in[r], fills(k, r))
                if not (isinstance(k, int) and k == 0):
                    pe.wait_ge(xT_out, k)
                for c in range(DC):
                    mm = nc.tensor.transpose(xTp[:, c * P:(c + 1) * P], xin[r][:, c * P:(c + 1) * P], ident[:])
                mm.then_inc(xT_full, 1)

            def fills(k, r):
                return 16 * (k // 2 + 1) if isinstance(k, int) else (k - r) * 8 + 16

            def gate_up(k, r, half, e):
                if half == 0:
                    pe.wait_ge(xT_out, k + 1)
                    if not (isinstance(k, int) and k < 2):
                        pe.wait_ge(hid_ready, k - 1)
                ps = (G, U)[half][r]
                for c in range(DC):
                    mm = nc.tensor.matmul(ps[:, 0:I], xinT[r][:, c * P:(c + 1) * P],
                                          wgu[:, bass.ds(e * (DC * GU) + (c * GU + half * I), I)],
                                          start=(c == 0), stop=(c == DC - 1))
                mm.then_inc((g_full, gu_full)[half], 1)

            def h_transpose(k, r):
                pe.wait_ge(hid_ready, k + 1)
                if not (isinstance(k, int) and k == 0):
                    pe.wait_ge(hT_out, k)
                for n, (o, w) in enumerate(IC):
                    mm = nc.tensor.transpose(hTp[0:w, n * P:(n + 1) * P], hid[r][:, o:o + w], ident[:])
                mm.then_inc(hT_full, 1)

            def down(k, r, e):
                pe.wait_ge(hT_out, k + 1)
                if not (isinstance(k, int) and k < 2):
                    pe.wait_ge(y_out, k - 1)
                for n, (o, w) in enumerate(IC):
                    mm = nc.tensor.matmul(Y[r][:], hidT[r][0:w, n * P:(n + 1) * P],
                                          wd[0:w, bass.ds(e * (len(IC) * D) + n * D, D)],
                                          start=(n == 0), stop=(n == len(IC) - 1))
                mm.then_inc(y_full, 1)

            def step(k, r, last=False):
                if not last:
                    e1 = expert(k + 1)
                    gate_up(k + 1, 1 - r, 0, e1)
                h_transpose(k, r)
                if not last:
                    gate_up(k + 1, 1 - r, 1, e1)
                down(k, r, expert(k))

            x_transpose(0, 0)
            pe.wait_ge(w_in, 16 * NW)
            x_transpose(1, 1)
            e0 = expert(0)
            gate_up(0, 0, 0, e0)
            gate_up(0, 0, 1, e0)

            def pair(m):
                for r in range(2):
                    k = m * 2 + r
                    x_transpose(k + 2, r)
                    step(k, r)

            pair(0)
            with nc.tensor.Fori(1, MT // 2 - 1) as m:
                pair(m)
            step(MT - 2, 0)
            step(MT - 1, 1, last=True)

        @block.vector
        def _(dve):
            def hidden(k, r):
                dve.wait_ge(silu_done, k + 1)
                dve.wait_ge(gu_full, k + 1)
                if not (isinstance(k, int) and k < 2):
                    dve.wait_ge(hT_full, k - 1)
                nc.vector.tensor_tensor(hid[r][:], U[r][:, 0:I], sg[r][:], ALU.mult).then_inc(hid_ready, 1)

            def take_hT(k, r):
                dve.wait_ge(hT_full, k + 1)
                if not (isinstance(k, int) and k < 2):
                    dve.wait_ge(y_full, k - 1)
                nc.vector.tensor_copy(hidT[r][:, 0:2 * P], hTp[:, 0:2 * P])
                w = I - 2 * P
                nc.vector.tensor_copy(hidT[r][0:w, 2 * P:3 * P], hTp[0:w, 2 * P:3 * P]).then_inc(hT_out, 1)

            def take_y(k, r):
                dve.wait_ge(y_full, k + 1)
                if not (isinstance(k, int) and k < 2):
                    dve.wait_ge(y_stored[r], 16 * (k // 2) if isinstance(k, int) else (k - r) * 8)
                nc.vector.tensor_copy(yo[r][:], Y[r][:]).then_inc(y_out, 1)

            hidden(0, 0)
            take_hT(0, 0)

            def pair(m):
                for r in range(2):
                    k = m * 2 + r
                    hidden(k + 1, 1 - r)
                    take_y(k, r)
                    take_hT(k + 1, 1 - r)

            pair(0)
            with nc.vector.Fori(1, MT // 2 - 1) as m:
                pair(m)
            hidden(MT - 1, 1)
            take_y(MT - 2, 0)
            take_hT(MT - 1, 1)
            take_y(MT - 1, 1)


def combine_block(nc, x1_dram, ys_dram, slots, wts, out):
    NTT = N // P
    with ExitStack() as ctx:
        def sb(name, shape, dt=F32):
            return ctx.enter_context(nc.sbuf_tensor(name, shape, dt))

        def sem(name):
            return ctx.enter_context(nc.semaphore(name))

        G = 4
        ya = [sb(f"ya{r}", [P, TOPK, D]) for r in range(G)]
        xr = [sb(f"xr{r}", [P, D]) for r in range(G)]
        res = [sb(f"res{r}", [P, D]) for r in range(G)]
        idx = [sb(f"cidx{r}", [P, TOPK], U32) for r in range(G)]
        bs = [sb(f"bs{r}", [P, 6]) for r in range(G)]
        mv = [sb(f"cmv{r}", [P, 2]) for r in range(G)]
        sd = [sb(f"sd{r}", [P, 1]) for r in range(G)]
        rs = [sb(f"rs{r}", [P, 1]) for r in range(G)]
        eps_t = sb("ceps", [P, 1])
        gathered = [sem(f"gathered{r}") for r in range(G)]
        x_in = [sem(f"cx_in{r}") for r in range(G)]
        idx_ready = sem("cidx_ready")
        summed = sem("summed")
        mv_ready = sem("cmv_ready")
        sd_ready = sem("sd_ready")
        chain = sem("cchain")
        eps_set = sem("eps_set")
        done = sem("cdone")
        stored = [sem(f"stored{r}") for r in range(G)]
        waited = sem("cwaited")

        def apart(e):
            e.sem_inc(waited, 1)

        block = ctx.enter_context(nc.Block())
        rounds = NTT // G
        out_f = out.rearrange("b t d -> (b t) d")

        @block.sync
        def _(sp):
            with nc.sync.Fori(0, rounds) as m:
                for r in range(G):
                    t = m * G + r
                    sp.wait_ge(idx_ready, t + 1)
                    sp.dma_start(xr[r][:], x1_dram[bass.ds(t * P, P), :]).then_inc(x_in[r], 16)

        @block.gpsimd
        def _(pool):
            def gather(t, r, wait):
                if wait:
                    pool.wait_ge(summed, t - G + 1)
                    apart(pool)
                nc.gpsimd.tensor_copy(idx[r][:], slots[:, bass.ds(t, 1), :].rearrange("p a k -> p (a k)")) \
                  .then_inc(idx_ready, 1)
                pool.wait_ge(idx_ready, t + 1)
                apart(pool)
                for k in range(TOPK):
                    nc.gpsimd.indirect_dma_start(ya[r][:, k, :], None, ys_dram,
                                                 bass.IndirectOffsetOnAxis(ap=idx[r][:, k:k + 1], axis=0)) \
                      .then_inc(gathered[r], 16)

            for r in range(G):
                gather(r, r, False)
            with nc.gpsimd.Fori(1, rounds) as m:
                for r in range(G):
                    gather(m * G + r, r, True)

        @block.scalar
        def _(act):
            def root(t, r):
                act.wait_ge(mv_ready, t + 1)
                nc.scalar.activation(sd[r][:], mv[r][:, 1:2], ACT.Sqrt, bias=eps_t[:, 0:1]).then_inc(sd_ready, 1)

            def store(t, r):
                act.wait_ge(done, t + 1)
                act.dma_start(out_f[bass.ds(t * P, P), :], res[r][:]).then_inc(stored[r], 16)

            act.wait_ge(eps_set, 1)
            with nc.scalar.Fori(0, rounds) as m:
                for r in range(G):
                    root(m * G + r, r)
                    store(m * G + r, r)
            for r in range(G):
                act.wait_ge(stored[r], 16 * rounds)

        @block.vector
        def _(dve):
            CH = 4
            nc.vector.memset(eps_t[:], EPS).then_inc(eps_set, 1)

            def tile(m, r, wait):
                t = m * G + r
                base = t * CH
                w = wts[:, bass.ds(t, 1), :].rearrange("p a k -> p (a k)")
                dve.wait_ge(gathered[r], 32 * (m + 1))
                dve.wait_ge(x_in[r], 16 * (m + 1))
                if wait:
                    dve.wait_ge(stored[r], 16 * m)
                nc.vector.scalar_tensor_tensor(out=res[r][:], in0=ya[r][:, 0, :], scalar=w[:, 0:1], in1=xr[r][:],
                                               op0=ALU.mult, op1=ALU.add).then_inc(chain, 1)
                dve.wait_ge(chain, base + 1)
                nc.vector.scalar_tensor_tensor(out=res[r][:], in0=ya[r][:, 1, :], scalar=w[:, 1:2], in1=res[r][:],
                                               op0=ALU.mult, op1=ALU.add).then_inc(summed, 1)
                dve.wait_ge(summed, t + 1)
                nc.vector.bn_stats(out=bs[r][:], in_=res[r][:]).then_inc(chain, 1)
                dve.wait_ge(chain, base + 2)
                apart(dve)
                nc.vector.bn_aggr(mv[r][:], bs[r][:]).then_inc(mv_ready, 1)
                dve.wait_ge(sd_ready, t + 1)
                nc.vector.reciprocal(rs[r][:], sd[r][:]).then_inc(chain, 1)
                dve.wait_ge(chain, base + 3)
                nc.vector.tensor_scalar(res[r][:], res[r][:], mv[r][:, 0:1], rs[r][:, 0:1],
                                        ALU.subtract, ALU.mult).then_inc(done, 1)
                dve.wait_ge(done, t + 1)
                nc.vector.nop().then_inc(chain, 1)

            for r in range(G):
                tile(0, r, False)
            with nc.vector.Fori(1, rounds) as m:
                for r in range(G):
                    tile(m, r, True)


def kernel(L0_attn_x, L0_attn_Wq, L0_attn_Wk, L0_attn_Wv, L0_attn_Wo, L0_attn_lambda_q1, L0_attn_lambda_k1,
           L0_attn_lambda_q2, L0_attn_lambda_k2, L0_attn_gn_w, L0_attn_gn_b, L0_ffn_gate_w, L0_ffn_w_gate,
           L0_ffn_w_up, L0_ffn_w_down):
    import concourse.bacc as _bacc
    from concourse.bass_utils import run_bass_kernel_spmd as _run
    import ml_dtypes

    def c(a):
        return np.ascontiguousarray(np.asarray(a))

    x = c(L0_attn_x)
    Wq, Wk, Wv = (c(a).reshape(DC, P, KV, -1) for a in (L0_attn_Wq, L0_attn_Wk, L0_attn_Wv))
    arrays = {
        "x": x,
        "xT": c(x.reshape(B, T, DC, P).transpose(3, 0, 2, 1)),
        "wqkv": c(np.concatenate([Wq, Wk, Wv], axis=3).transpose(1, 0, 2, 3)),
        "wo": c(c(L0_attn_Wo).reshape(FC, P, D).transpose(1, 0, 2)),
        "lam": c(np.stack([c(L0_attn_lambda_q1), c(L0_attn_lambda_k1), c(L0_attn_lambda_q2), c(L0_attn_lambda_k2)])),
        "gnw": c(c(L0_attn_gn_w).reshape(FC, P).T),
        "gnb": c(c(L0_attn_gn_b).reshape(FC, P).T),
        "gate": c(c(L0_ffn_gate_w).T.reshape(DC, P, E).transpose(1, 0, 2)),
        "wg": c(L0_ffn_w_gate),
        "wu": c(L0_ffn_w_up),
        "wd": c(L0_ffn_w_down),
    }
    inv = (np.float32(1.0) / np.power(np.float32(10000.0), np.arange(0, DH, 2, dtype=np.float32) / np.float32(DH))).astype(np.float32)
    fr = (np.arange(T, dtype=np.float32)[:, None] * inv[None, :]).astype(np.float32)
    for name, f in (("rope_cos", np.cos), ("rope_sin", np.sin)):
        t = f(fr.astype(np.float64)).reshape(NT, P, 1, DH // 2).transpose(1, 0, 2, 3)
        q = np.broadcast_to(t / math.sqrt(DH), (P, NT, 2 * RK, DH // 2))
        k = np.broadcast_to(t, (P, NT, 2, DH // 2))
        arrays[name] = c(np.concatenate([q, k], axis=2).astype(np.float32))
    eye = np.eye(P, dtype=np.float32)
    arrays["ident"] = eye
    arrays["identb"] = eye.astype(ml_dtypes.bfloat16)
    arrays["maskb"] = np.where(np.arange(P)[None, :] > np.arange(P)[:, None], NEG, 0.0).astype(ml_dtypes.bfloat16)
    arrays["tri"] = (np.arange(P)[:, None] < np.arange(P)[None, :]).astype(np.float32)
    same = np.arange(P)[:, None] // HD == np.arange(P)[None, :] // HD
    arrays["avg"] = (same / HD).astype(np.float32)
    en = np.arange(E, dtype=np.float32)
    arrays["small"] = c(np.broadcast_to(np.stack([en, en * R])[None, :, None, :], (P, 2, NT, E)))
    region = en[None, :] * R + np.arange(P, dtype=np.float32)[:, None]
    incl = (np.arange(E)[None, :] <= np.arange(E)[:, None]).astype(np.float32).reshape(1, -1)
    kio = np.repeat(np.arange(MT, dtype=np.float32), E).reshape(1, -1)
    rest = np.concatenate([np.zeros((1, E), np.float32), incl, kio, kio], axis=1)
    arrays["plan"] = c(np.concatenate([region, np.broadcast_to(rest, (P, rest.shape[1]))], axis=1).astype(np.float32))

    nc = _bacc.Bacc("TRN2", target_bir_lowering=False, num_devices=1)
    names = ["x", "xT", "wqkv", "wo", "lam", "gnw", "gnb", "gate", "wg", "wu", "wd", "rope_cos", "rope_sin",
             "ident", "identb", "maskb", "tri", "avg", "small", "plan"]
    args = [nc.dram_tensor(f"in_{n}", arrays[n].shape, mybir.dt.from_np(arrays[n].dtype), kind="ExternalInput").ap()
            for n in names]
    o = nc.dram_tensor("out_y", (B, T, D), F32, kind="ExternalOutput").ap()
    layer_kernel(nc, *args, o)
    r = _run(nc, [{f"in_{n}": arrays[n] for n in names}], core_ids=[0])
    return r.results[0]["out_y"]
```

```python
from contextlib import ExitStack
import math

import numpy as np

import concourse.bass as bass
from concourse import mybir

F32 = mybir.dt.float32
F32R = mybir.dt.float32r
BF16 = mybir.dt.bfloat16
I32 = mybir.dt.int32
U32 = mybir.dt.uint32
ALU = mybir.AluOpType
ACT = mybir.ActivationFunctionType
AX = mybir.AxisListType.X

P = 128
B, T, D = 8, 512, 512
H, KV, DH = 16, 4, 32
HD = 2 * DH
RK = H // KV
NT = T // P
DC = D // P
FC = H * HD // P
CQ = RK * HD + 2 * HD
NG = 2 * RK + 2
E, TOPK, I = 8, 2, 352
N = B * T
R = N + P
MT = (TOPK * N + E * (P - 1)) // P + 1
MT += MT % 2
IC = [(o, min(P, I - o)) for o in range(0, I, P)]
EARLY = 8
EPS = 1e-5
LAMBDA_INIT = 0.8 - 0.6 * math.exp(-0.3 * 0)
NEG = -3.0e38

UNITS = [(0, (0, 1)), (0, (2, 3)), (1, (0, 1)), (1, (2, 3))] + [(i, (h,)) for i in (2, 3) for h in range(RK)]
NU = len(UNITS)
UB = NU * KV
assert UB % 6 == 0

LAG_T, LAG_V = 3, 4

PREP = {0: [("proj", 0)], 2: [("proj", 1)], 3: [("stack", 0)], 4: [("proj", 2)], 5: [("stack", 1)], 6: [("proj", 3)],
        7: [("stack", 2), ("stack", 3)], 8: [("stack", 4), ("stack", 5)], 9: [("stack", 6), ("stack", 7)],
        10: [("stack", 8)], 11: [("stack", 9)]}
PREP_ORDER = [x for s in sorted(PREP) for x in PREP[s]]
PREP_N = len(PREP_ORDER)
PREP_LEAD = 2 * NT + NG

TAIL_PE = {c + 3: [("ctxT", c)] for c in range(FC)}
TAIL_PE[13] = [("gn", 0)]
OP0 = 20
for _i in range(NT):
    for _q in range(4):
        TAIL_PE[OP0 + 4 * _i + _q] = [("oproj", _i, _q)]
TAIL_PE[OP0 + 20] = [("xT", 0)]
TAIL_PE[OP0 + 21] = [("xT", 1)]
TAIL_PE[OP0 + 22] = [("xT", 2)]
TAIL_PE[OP0 + 23] = [("xT", 3)]
TAIL_PE[OP0 + 24] = [("logits", 0)]
TAIL_PE[OP0 + 26] = [("rank", 0)]
TAIL_ORDER = [("ctxT", c) for c in range(FC)] + [("gn", 0)] + [("oproj", i) for i in range(NT)] \
    + [("xT", i) for i in range(NT)] + [("logits", 0), ("rank", 0)]
TAIL_N = len(TAIL_ORDER)


def layer_kernel(nc, x, xT_d, wqkv_d, wo_d, lam_d, gnw_d, gnb_d, gate_d, wg_d, wu_d, wd_d,
                 rope_cos_d, rope_sin_d, ident_d, identb_d, maskb_d, tri_d, avg_d, small_d, plan_d, out):
    x1_dram = nc.dram_tensor("x1_rows", [N, D], F32, kind="Internal").ap()
    xs_dram = nc.dram_tensor("expert_in_rows", [E * R, D], F32, kind="Internal").ap()
    ys_dram = nc.dram_tensor("expert_out_rows", [MT * P, D], F32, kind="Internal").ap()
    wsplit_dram = nc.dram_tensor("wqkv_split", [P, KV, DC, 2, CQ], F32, kind="Internal").ap()

    with ExitStack() as keep:
        def sbk(name, shape, dt=F32):
            return keep.enter_context(nc.sbuf_tensor(name, shape, dt))

        ident = sbk("ident", [P, P])
        ones = sbk("ones", [P, P])
        slots = sbk("slots", [P, N // P, TOPK], U32)
        wts = sbk("wts", [P, N // P, TOPK])
        msum = sbk("msum", [P, E])
        exp_tab = sbk("exp_tab", [1, MT], I32)
        row_tab = sbk("row_tab", [1, MT], I32)
        out_slots = sbk("out_slots", [P, N // P, TOPK], U32)
        attention_block(nc, x, xT_d, wqkv_d, wo_d, lam_d, gnw_d, gnb_d, gate_d, rope_cos_d, rope_sin_d,
                        ident_d, identb_d, maskb_d, tri_d, avg_d, small_d, x1_dram, xs_dram, wsplit_dram,
                        ident, ones, slots, wts, msum)
        x_early = sbk("x_early", [P, EARLY, D])
        x_early_in = keep.enter_context(nc.semaphore("x_early_in"))
        with ExitStack() as weights:
            wgu = weights.enter_context(nc.sbuf_tensor("wgu", [P, E * DC * 2 * I], F32))
            wd = weights.enter_context(nc.sbuf_tensor("wd", [P, E * len(IC) * D], F32))
            ew_in = [weights.enter_context(nc.semaphore(f"expert_w_in{e}")) for e in range(E)]
            wgu_v = wgu[:].rearrange("p (e c g i) -> p e c g i", e=E, c=DC, g=2)
            wd_v = wd[:].rearrange("p (e c d) -> p e c d", e=E, c=len(IC))

            def load_weights(sp, e):
                for g, w in enumerate((wg_d, wu_d)):
                    sp.dma_start(wgu_v[:, e, :, g, :], w[e].rearrange("(c p) i -> p c i", p=P)).then_inc(ew_in[e], 16)
                sp.dma_start(wd_v[:, e, 0:2, :], wd_d[e, 0:2 * P].rearrange("(c p) d -> p c d", p=P)).then_inc(ew_in[e], 16)
                sp.dma_start(wd_v[0:I - 2 * P, e, 2, :], wd_d[e, 2 * P:I]).then_inc(ew_in[e], 16)

            plan_block(nc, plan_d, load_weights, xs_dram, ones, msum, slots, out_slots,
                       exp_tab, row_tab)
            expert_block(nc, wgu, wd, ew_in, load_weights, xs_dram, ys_dram, x1_dram, x_early, x_early_in, ident, exp_tab, row_tab)
        combine_block(nc, x1_dram, ys_dram, out_slots, wts, x_early, x_early_in, out)


def attention_block(nc, x, xT_d, wqkv_d, wo_d, lam_d, gnw_d, gnb_d, gate_d, rope_cos_d, rope_sin_d,
                    ident_d, identb_d, maskb_d, tri_d, avg_d, small_d, x1_dram, xs_dram, wsplit_dram,
                    ident, ones, slots, wts, msum):
    with ExitStack() as ctx:
        def sb(name, shape, dt=F32):
            return ctx.enter_context(nc.sbuf_tensor(name, shape, dt))

        def pb(name, shape, dt=F32):
            return ctx.enter_context(nc.psum_tensor(name, shape, dt))

        def sem(name):
            return ctx.enter_context(nc.semaphore(name))

        wqkv = [sb(f"wqkv{r}", [P, DC, 2, CQ], F32R) for r in range(2)]
        wo = sb("wo", [P, FC, D])
        gate = sb("gate", [P, DC, E])
        rcos = sb("rcos", [P, NT, 2, DH // 2])
        rsin = sb("rsin", [P, NT, 2, DH // 2])
        identb = sb("identb", [P, P], BF16)
        maskb = sb("maskb", [P, P], BF16)
        tri = sb("tri", [P, P])
        avg = sb("avg", [P, P])
        gnw = sb("gnw", [P, FC])
        gnb = sb("gnb", [P, FC])
        small = sb("small", [P, 2, NT, E])
        lam_in = sb("lam_in", [P, 4, DH])
        lam_pr = sb("lam_pr", [P, 2, DH])
        lam_s = sb("lam_s", [P, 2])
        lam_e = sb("lam_e", [P, 2])
        neg_lam = sb("neg_lam", [P, 1])
        eps_t = sb("eps_t", [P, 1])
        xh = sb("xh", [P, DC, T], F32R)
        xl = sb("xl", [P, DC, T], F32R)
        qkv = sb("qkv", [P, NT, CQ])
        ra = sb("ra", [P, NT, NG, DH // 2])
        rb = sb("rb", [P, NT, NG, DH // 2])
        roped = sb("roped", [P, NT, NG, DH])
        split = sb("split", [P, NT * NG, P])
        qT = [sb(f"qT{r}", [P, 2 * RK, T], F32R) for r in range(2)]
        kT = [sb(f"kT{r}", [P, 2, T], F32R) for r in range(2)]
        vals = [sb(f"vals{r}", [P, NT, HD]) for r in range(KV)]
        neg_max = [sb(f"neg_max{r}", [P, 4]) for r in range(3)]
        sums = [sb(f"sums{r}", [P, NT, 2, RK]) for r in range(2)]
        rsum = [sb(f"rsum{r}", [P, NT, 2, RK]) for r in range(2)]
        rho = [sb(f"rho{r}", [P, NT, RK]) for r in range(2)]
        expd = [sb(f"expd{r}", [P, 1024]) for r in range(3)]
        mixed = [sb(f"mixed{r}", [P, 512]) for r in range(3)]
        probsT = [sb(f"probsT{r}", [P, 512]) for r in range(2)]
        ctxn = sb("ctxn", [P, NT, H * HD])
        ctxT = sb("ctxT", [P, FC, T])
        bn = sb("bn", [P, FC, 6])
        st = sb("st", [P, FC, 2])
        st2 = sb("st2", [P, FC, 2])
        gst = sb("gst", [P, FC, 2])
        gvar = sb("gvar", [P, FC])
        gsd = sb("gsd", [P, FC])
        grs = sb("grs", [P, FC])
        gsc = sb("gsc", [P, FC])
        gms = sb("gms", [P, FC])
        gbi = sb("gbi", [P, FC])
        x1 = sb("x1", [P, NT, D])
        bx = sb("bx", [P, NT, 6])
        mv = sb("mv", [P, NT, 2])
        xsd = sb("xsd", [P, NT])
        xrs = sb("xrs", [P, NT])
        lg = sb("lg", [P, NT, E])
        top = sb("top", [P, NT, E])
        topi = sb("topi", [P, NT, E], U32)
        topf = sb("topf", [P, NT, 2])
        pick = sb("pick", [P, 2, NT, E])
        member = sb("member", [P, NT, E])
        msum_t = sb("msum_t", [P, E])
        rank = sb("rank", [P, NT, E])
        pr = sb("pr", [P, 2, NT, E])
        slotf = sb("slotf", [P, TOPK, NT])
        dl = sb("dl", [P, NT])
        ed = sb("ed", [P, NT])
        ed1 = sb("ed1", [P, NT])

        S = [pb(f"S{r}", [P, 1024]) for r in range(2)]
        PTp = pb("PTp", [P, 512])
        O = pb("O", [P, RK, HD])
        prep = pb("prep", [P, 512])
        tail = pb("tail", [P, 512])

        consts_in = sem("consts_in")
        lam_step = sem("lam_step")
        lam_exp = sem("lam_exp")
        lam_ready = sem("lam_ready")
        xT_in = sem("xT_in")
        xh_ready = sem("xh_ready")
        xl_ready = sem("xl_ready")
        wraw_in = sem("wraw_in")
        wh_ready = sem("wh_ready")
        wl_ready = sem("wl_ready")
        wsplit_stored = sem("wsplit_stored")
        w_in = [sem(f"wqkv_in{r}") for r in range(2)]
        prep_full = sem("prep_full")
        prep_out = sem("prep_out")
        rope_step = sem("rope_step")
        rope_done = sem("rope_done")
        vals_ready = sem("vals_ready")
        hi_done = sem("hi_done")
        split_done = sem("split_done")
        scores_ready = sem("scores_ready")
        max_ready = sem("max_ready")
        exp_done = sem("exp_done")
        rsum_step = sem("rsum_step")
        rho_step = sem("rho_step")
        mix_ready = sem("mix_ready")
        pT_full = sem("pT_full")
        pT_out = sem("pT_out")
        ctx_full = sem("ctx_full")
        ctx_scaled = sem("ctx_scaled")
        tail_full = sem("tail_full")
        tail_act = sem("tail_act")
        tail_dve = sem("tail_dve")
        t_step = sem("t_step")
        gvar_ready = sem("gvar_ready")
        gsd_ready = sem("gsd_ready")
        norm_ready = sem("norm_ready")
        st_ready = sem("st_ready")
        x_in = sem("x_in")
        mv_ready = sem("mv_ready")
        xsd_ready = sem("xsd_ready")
        x1_ready = sem("x1_ready")
        member_ready = sem("member_ready")
        dl_ready = sem("dl_ready")
        ed_ready = sem("ed_ready")
        slots_ready = sem("slots_ready")
        x1_stored = sem("x1_stored")
        scattered = sem("scattered")
        NCONST = 13

        block = ctx.enter_context(nc.Block())

        waited = sem("waited")

        def apart(e):
            e.sem_inc(waited, 1)

        def at_least(e, s, v):
            if not isinstance(v, int) or v > 0:
                e.wait_ge(s, v)

        wraw = [w[:].rearrange("p a b -> p (a b)")[:, k * DC * CQ:(k + 1) * DC * CQ].rearrange("p (c f) -> p c f", c=DC)
                for w in (ctxn, ctxT) for k in range(2)]
        wparts = [w[:] for w in wqkv] + [
            w[:].rearrange("p a b -> p (a b)")[:, 0:DC * 2 * CQ].rearrange("p (c s f) -> p c s f", c=DC, s=2) for w in qT]

        def prep_count(b, kv, kind, j, last=False):
            n = PREP_ORDER.index((kind, j))
            less = sum(k == "proj" for k, _ in PREP_ORDER[:n]) if last and kv == KV - 2 else 0
            return PREP_LEAD + PREP_N * (b * KV + kv) + n + 1 - less

        def tail_count(b, *task):
            return b * TAIL_N + TAIL_ORDER.index(task) + 1

        ACT_TAIL = [("ctxT", c) for c in range(FC)] + [("xT", i) for i in range(NT)]
        DVE_TAIL = [("gn", 0)] + [("oproj", i) for i in range(NT)] + [("logits", 0), ("rank", 0)]

        def tail_bank_free(e, b, *task):
            n = TAIL_ORDER.index(task)
            if n == 0:
                return
            before = TAIL_ORDER[n - 1]
            if before in ACT_TAIL:
                e.wait_ge(tail_act, b * len(ACT_TAIL) + ACT_TAIL.index(before) + 1)
            else:
                e.wait_ge(tail_dve, b * len(DVE_TAIL) + DVE_TAIL.index(before) + 1)

        def batches(eng, body, end):
            body(0, True, False)
            with eng.Fori(1, B - 1) as b:
                body(b, False, False)
            body(B - 1, False, True)
            end(B)

        def steps(b, first, last):
            for s in range(UB):
                yield s, s // NU, b * UB + s

        def lagged(b, s, lag, first):
            if first and s < lag:
                return None
            return (s - lag) % UB, b * UB + s - lag

        def preps(s, kv, last):
            for kind, j in PREP.get(s % NU, []):
                if last and (kv == KV - 1 or (kv == KV - 2 and kind == "proj")):
                    continue
                yield kind, j

        @block.sync
        def _(sp):
            sp.dma_start(x1[:], xT_d[:, 0]).then_inc(xT_in, 16)
            for kv in range(KV):
                sp.dma_start(wraw[kv], wqkv_d[:, :, kv, :]).then_inc(wraw_in, 16)
            for dst, src in ((ident[:], ident_d), (rcos[:], rope_cos_d),
                             (rsin[:], rope_sin_d), (lam_in[:], lam_d.unsqueeze(0).broadcast_to([P, 4, DH])),
                             (identb[:], identb_d), (maskb[:], maskb_d), (avg[:], avg_d), (tri[:], tri_d),
                             (gnw[:], gnw_d), (gnb[:], gnb_d), (small[:], small_d), (gate[:], gate_d),
                             (wo[:], wo_d)):
                sp.dma_start(dst, src).then_inc(consts_in, 16)
            sp.wait_ge(wl_ready, KV)
            for kv in range(KV):
                sp.dma_start(wsplit_dram[:, kv], wparts[kv].bitcast(F32)).then_inc(wsplit_stored, 16)

            def load_x(b):
                sp.dma_start(x1[:], x[b].rearrange("(i p) d -> p i d", p=P)).then_inc(x_in, 16)

            def store_x1(b):
                sp.wait_ge(x1_ready, NT * (b + 1))
                sp.dma_start(x1_dram[bass.ds(b * T, T), :].rearrange("(i p) d -> p i d", p=P), x1[:]) \
                  .then_inc(x1_stored, 16)
                sp.wait_ge(x1_stored, 16 * (b + 1))
                apart(sp)
                sp.wait_ge(scattered, 16 * NT * TOPK * (b + 1))
                apart(sp)

            def body(b, first, last):
                if not last:
                    sp.wait_ge(prep_full, prep_count(b, 1, "proj", NT - 1))
                    sp.dma_start(x1[:], xT_d[:, b + 1]).then_inc(xT_in, 16)
                    sp.wait_ge(xl_ready, b + 2)
                if not first:
                    load_x(b - 1)
                if not first:
                    store_x1(b - 1)

            def end(b):
                load_x(b - 1)
                store_x1(b - 1)

            batches(nc.sync, body, end)

        @block.gpsimd
        def _(pool):
            ROPE_OPS = 12

            def times(out_, in_, table):
                for kind, g0, g1 in ((0, 0, 2 * RK), (1, 2 * RK, NG)):
                    tab = table[:, :, kind:kind + 1, :].broadcast_to([P, NT, g1 - g0, DH // 2])
                    nc.gpsimd.tensor_tensor(out_[:, :, g0:g1], in_[:, :, g0:g1], tab, ALU.mult).then_inc(rope_step, 1)

            def rope(n, kv, first_ever=False):
                pool.wait_ge(prep_out, proj_out(n))
                if not (isinstance(n, int) and n == 0):
                    pool.wait_ge(hi_done, n)
                xe = qkv[:, :, 0:NG * DH].rearrange("p t (g j two) -> p t g j two", g=NG, two=2)
                oe = roped[:].rearrange("p t g (j two) -> p t g j two", two=2)
                x0, x1_ = xe[:, :, :, :, 0], xe[:, :, :, :, 1]
                base = n * ROPE_OPS
                if not (isinstance(n, int) and n < KV):
                    pool.wait_ge(ctx_full, (n - KV + 1) * NU)
                apart(pool)
                nc.gpsimd.tensor_copy(vals[kv][:], qkv[:, :, NG * DH:CQ]).then_inc(vals_ready, 1)
                times(ra, x0, rcos)
                times(rb, x1_, rsin)
                pool.wait_ge(rope_step, base + 4)
                nc.gpsimd.tensor_tensor(oe[:, :, :, :, 0], ra[:], rb[:], ALU.subtract).then_inc(rope_step, 1)
                pool.wait_ge(rope_step, base + 5)
                times(ra, x0, rsin)
                times(rb, x1_, rcos)
                pool.wait_ge(rope_step, base + 9)
                nc.gpsimd.tensor_tensor(oe[:, :, :, :, 1], ra[:], rb[:], ALU.add).then_inc(rope_done, 1)
                pool.wait_ge(hi_done, n + 1)
                r2 = roped[:].rearrange("p t g d -> p (t g) d")
                nc.gpsimd.tensor_tensor(split[:, :, 3 * DH:4 * DH], r2, split[:, :, 0:DH], ALU.subtract) \
                  .then_inc(rope_step, 1)
                pool.wait_ge(rope_step, base + 10)
                apart(pool)
                s4 = split[:].rearrange("p (t g) f -> p t g f", g=NG)
                nc.gpsimd.tensor_copy(s4[:, :, 0:2 * RK, 2 * DH:3 * DH], s4[:, :, 0:2 * RK, 3 * DH:4 * DH]) \
                  .then_inc(rope_step, 1)
                nc.gpsimd.tensor_copy(s4[:, :, 2 * RK:NG, DH:2 * DH], s4[:, :, 2 * RK:NG, 3 * DH:4 * DH]) \
                  .then_inc(rope_step, 1)
                pool.wait_ge(rope_step, base + 12)
                nc.gpsimd.nop().then_inc(split_done, 1)

            def proj_out(n):
                if isinstance(n, int) and n < 2:
                    return NT * (n + 1)
                return PREP_LEAD + PREP_N * (n - 2) + PREP_ORDER.index(("proj", NT - 1)) + 1

            def load_w(slot, head):
                nc.gpsimd.dma_start(wqkv[slot][:], wsplit_dram[:, head]).then_inc(w_in[slot], 16)

            def scatter(b):
                for i in range(NT):
                    for k in range(TOPK):
                        nc.gpsimd.indirect_dma_start(
                            xs_dram, bass.IndirectOffsetOnAxis(ap=idx[:, i, k:k + 1], axis=0), x1[:, i, :], None,
                        ).then_inc(scattered, 16)

            idx = sb("idx", [P, NT, TOPK], U32)
            idx_copied = sem("idx_copied")

            def body(b, first, last):
                for kv in range(KV):
                    if not last:
                        pool.wait_ge(prep_out, proj_out(b * KV + kv + 2))
                        apart(pool)
                        load_w(kv % 2, kv)
                    if not (last and kv >= KV - 2):
                        rope(b * KV + kv + 2, (kv + 2) % KV)
                if not first:
                    send(b - 1)

            def send(b):
                pool.wait_ge(slots_ready, b + 1)
                apart(pool)
                nc.gpsimd.tensor_copy(idx[:], slots[:, bass.ds(b * NT, NT), :]).then_inc(idx_copied, 1)
                pool.wait_ge(idx_copied, b + 1)
                pool.wait_ge(x1_ready, NT * (b + 1))
                apart(pool)
                scatter(b)

            def end(b):
                send(b - 1)
                pool.wait_ge(scattered, 16 * b * NT * TOPK)

            pool.wait_ge(consts_in, 16 * NCONST)
            pool.wait_ge(wsplit_stored, 16 * KV)
            pool.wait_ge(prep_out, proj_out(0))
            load_w(0, 2)
            rope(0, 0)
            pool.wait_ge(prep_out, proj_out(1))
            load_w(1, 3)
            rope(1, 1)
            batches(nc.gpsimd, body, end)

        @block.tensor
        def _(pe):
            def proj(n_kv, t, count):
                at_least(pe, prep_out, count - 1)
                here = slice(t * P, (t + 1) * P)
                w = wqkv[n_kv % 2]
                for c in range(DC):
                    nc.tensor.matmul(prep[:, 0:CQ], xh[:, c, here], w[:, c, 0, :], start=(c == 0), stop=False)
                    nc.tensor.matmul(prep[:, 0:CQ], xh[:, c, here], w[:, c, 1, :], start=False, stop=False)
                    mm = nc.tensor.matmul(prep[:, 0:CQ], xl[:, c, here], w[:, c, 0, :], start=False, stop=(c == DC - 1))
                mm.then_inc(prep_full, 1)

            def stack(g, count):
                at_least(pe, prep_out, count - 1)
                for t in range(NT):
                    mm = nc.tensor.transpose(prep[:, t * P:(t + 1) * P], split[:, t * NG + g, :], ident[:])
                mm.then_inc(prep_full, 1)

            def scores(b, s, u, kv):
                i, heads = UNITS[s % NU]
                n = b * KV + kv
                if s % NU == 0:
                    pe.wait_ge(prep_out, stack_out(n))
                at_least(pe, exp_done, u - 1)
                slot, w = (256, 256) if i < 2 else (512, P * (i + 1))
                for a, h in enumerate(heads):
                    for c in range(2):
                        o = (2 * a + c) * slot
                        nc.tensor.matmul(S[s % 2][:, o:o + w], qT[kv % 2][:, 2 * h + c, i * P:(i + 1) * P],
                                         kT[kv % 2][:, c, 0:w], start=True, stop=False)
                        mm = nc.tensor.matmul(S[s % 2][:, o + i * P:o + (i + 1) * P], identb[:], maskb[:],
                                              start=False, stop=True)
                mm.then_inc(scores_ready, 1)

            def stack_out(n):
                if isinstance(n, int) and n == 0:
                    return PREP_LEAD
                less = NT if isinstance(n, int) and n == B * KV - 1 else 0
                return PREP_LEAD + PREP_N * (n - 1) + PREP_ORDER.index(("stack", NG - 1)) + 1 - less

            def transposes(sl, u):
                i, heads = UNITS[sl % NU]
                pe.wait_ge(mix_ready, u + 1)
                at_least(pe, pT_out, u)
                for a in range(len(heads)):
                    for j in range(i + 1):
                        o = (a * (i + 1) + j) * P
                        mm = nc.tensor.transpose(PTp[:, o:o + P], mixed[sl % 3][:, a * 256 + j * P:a * 256 + (j + 1) * P],
                                                 ident[:])
                mm.then_inc(pT_full, 1)

            def values(sl, u):
                i, heads = UNITS[sl % NU]
                kv = sl // NU
                pe.wait_ge(pT_out, u + 1)
                if heads[0] == 0:
                    at_least(pe, ctx_scaled, group_no(sl, u))
                for a, h in enumerate(heads):
                    for j in range(i + 1):
                        o = (a * (i + 1) + j) * P
                        mm = nc.tensor.matmul(O[:, h, :], probsT[sl % 2][:, o:o + P], vals[kv][:, j, :],
                                              start=(j == 0), stop=(j == i))
                mm.then_inc(ctx_full, 1)

            def group_no(sl, u):
                local = (sl // NU) * NT + UNITS[sl % NU][0]
                if isinstance(u, int):
                    return (u // UB) * KV * NT + local
                return batch_of(u, sl) * (KV * NT) + local

            batch_reg = [0]

            def batch_of(u, sl):
                return batch_reg[0] if sl < UB - LAG_V else batch_reg[0] - 1

            def tail_task(b, task):
                kind = task[0]
                if kind == "ctxT":
                    c = task[1]
                    if c % (FC // KV) == 0:
                        pe.wait_ge(ctx_scaled, (b * KV + c // (FC // KV) + 1) * NT)
                    tail_bank_free(pe, b, *task)
                    for i in range(NT):
                        mm = nc.tensor.transpose(tail[:, i * P:(i + 1) * P], ctxn[:, i, c * P:(c + 1) * P], ident[:])
                    mm.then_inc(tail_full, 1)
                elif kind == "gn":
                    pe.wait_ge(st_ready, b + 1)
                    tail_bank_free(pe, b, *task)
                    nc.tensor.matmul(tail[:, 0:2 * FC], avg[:], st2[:].rearrange("p c s -> p (c s)"),
                                     start=True, stop=True).then_inc(tail_full, 1)
                elif kind == "oproj":
                    i, q = task[1], task[2]
                    if q == 0:
                        pe.wait_ge(norm_ready, b + 1)
                        tail_bank_free(pe, b, "oproj", i)
                    for c in range(2 * q, 2 * q + 2):
                        mm = nc.tensor.matmul(tail[:], ctxT[:, c, i * P:(i + 1) * P], wo[:, c, :],
                                              start=(c == 0), stop=(c == FC - 1))
                    if q == 3:
                        mm.then_inc(tail_full, 1)
                elif kind == "xT":
                    i = task[1]
                    pe.wait_ge(x1_ready, b * NT + i + 1)
                    tail_bank_free(pe, b, *task)
                    for c in range(DC):
                        mm = nc.tensor.transpose(tail[:, c * P:(c + 1) * P], x1[:, i, c * P:(c + 1) * P], ident[:])
                    mm.then_inc(tail_full, 1)
                elif kind == "logits":
                    tail_bank_free(pe, b, *task)
                    for i in range(NT):
                        for c in range(DC):
                            mm = nc.tensor.matmul(tail[:, i * E:(i + 1) * E], ctxT[:, i, c * P:(c + 1) * P],
                                                  gate[:, c, :], start=(c == 0), stop=(c == DC - 1))
                    mm.then_inc(tail_full, 1)
                else:
                    pe.wait_ge(member_ready, b + 1)
                    tail_bank_free(pe, b, *task)
                    for i in range(NT):
                        o = tail[:, i * E:(i + 1) * E]
                        nc.tensor.matmul(o, ones[:], msum[:], start=True, stop=False)
                        for j in range(i):
                            nc.tensor.matmul(o, ones[:], member[:, j, :], start=False, stop=False)
                        mm = nc.tensor.matmul(o, tri[:], member[:, i, :], start=False, stop=True)
                    mm.then_inc(tail_full, 1)

            def body(b, first, last):
                batch_reg[0] = b
                for s, kv, u in steps(b, first, last):
                    scores(b, s, u, kv)
                    todo = list(preps(s, kv, last))

                    def prep_task():
                        if not todo:
                            return
                        kind, j = todo.pop(0)
                        count = prep_count(b, kv, kind, j, last)
                        if kind == "proj":
                            if j == 0 and kv == KV - 2:
                                pe.wait_ge(xl_ready, b + 2)
                            if j == 0:
                                pe.wait_ge(w_in[kv % 2], 16 * (b * (KV // 2) + (kv + 2) // 2))
                            proj((kv + 2) % KV, j, count)
                        else:
                            if j == 0:
                                pe.wait_ge(split_done, b * KV + kv + 2)
                            stack(j, count)

                    prep_task()
                    if lagged(b, s, LAG_T, first):
                        transposes(*lagged(b, s, LAG_T, first))
                    if lagged(b, s, LAG_V, first):
                        values(*lagged(b, s, LAG_V, first))
                    prep_task()
                    if not first:
                        for task in TAIL_PE.get(s, []):
                            tail_task(b - 1, task)

            def end(b):
                batch_reg[0] = b
                for s in range(LAG_V):
                    if s < LAG_T:
                        transposes(*lagged(b, s, LAG_T, False))
                    values(*lagged(b, s, LAG_V, False))
                for s in sorted(TAIL_PE):
                    for task in TAIL_PE[s]:
                        tail_task(b - 1, task)

            pe.wait_ge(consts_in, 16 * NCONST)
            pe.wait_ge(xl_ready, 1)
            for n in range(2):
                pe.wait_ge(wl_ready, n + 1)
                for t in range(NT):
                    proj(n, t, n * NT + t + 1)
            pe.wait_ge(split_done, 1)
            for g in range(NG):
                stack(g, 2 * NT + g + 1)
            pe.wait_ge(lam_ready, 1)
            batches(nc.tensor, body, end)

        @block.scalar
        def _(act):
            def take_proj(t, count, n):
                act.wait_ge(prep_full, count)
                if t == 0 and not (isinstance(n, int) and n == 0):
                    act.wait_ge(rope_done, n)
                nc.scalar.activation(qkv[:, t, :], prep[:, 0:CQ], ACT.Copy).then_inc(prep_out, 1)

            def take_stack(g, count, kvn):
                act.wait_ge(prep_full, count)
                dst = qT[kvn % 2][:, g, :] if g < 2 * RK else kT[kvn % 2][:, g - 2 * RK, :]
                nc.scalar.activation(dst, prep[:], ACT.Copy).then_inc(prep_out, 1)

            def exps(s, u):
                i, heads = UNITS[s % NU]
                kv = s // NU
                act.wait_ge(max_ready, u + 1)
                at_least(act, mix_ready, u - 2)
                slot, w = (256 if i < 2 else 512), P * (i + 1)
                for a, h in enumerate(heads):
                    for c in range(2):
                        k = 2 * a + c
                        ex = nc.scalar.activation(expd[s % 3][:, k * slot:k * slot + w], S[s % 2][:, k * slot:k * slot + w],
                                                  ACT.Exp, bias=neg_max[s % 3][:, k:k + 1], scale=1.0,
                                                  accum_out=sums[kv % 2][:, i, c, h:h + 1])
                ex.then_inc(exp_done, 1)

            def take_probsT(sl, u):
                i, heads = UNITS[sl % NU]
                w = len(heads) * (i + 1) * P
                act.wait_ge(pT_full, u + 1)
                at_least(act, ctx_full, u - 1)
                nc.scalar.activation(probsT[sl % 2][:, 0:w], PTp[:, 0:w], ACT.Copy).then_inc(pT_out, 1)

            def tail_task(b, task):
                kind = task[0]
                if kind == "ctxT":
                    c = task[1]
                    act.wait_ge(tail_full, tail_count(b, *task))
                    nc.scalar.activation(ctxT[:, c, :], tail[:], ACT.Copy).then_inc(tail_act, 1)
                elif kind == "xT":
                    act.wait_ge(tail_full, tail_count(b, *task))
                    nc.scalar.activation(ctxT[:, task[1], :], tail[:], ACT.Copy).then_inc(tail_act, 1)
                elif kind == "gn":
                    act.wait_ge(gvar_ready, b + 1)
                    nc.scalar.activation(gsd[:], gvar[:], ACT.Sqrt, bias=eps_t[:, 0:1]).then_inc(gsd_ready, 1)
                elif kind == "ln":
                    act.wait_ge(mv_ready, b + 1)
                    nc.scalar.activation(xsd[:], mv[:, :, 1], ACT.Sqrt, bias=eps_t[:, 0:1]).then_inc(xsd_ready, 1)
                elif kind == "wt":
                    act.wait_ge(dl_ready, b + 1)
                    nc.scalar.activation(ed[:], dl[:], ACT.Exp).then_inc(ed_ready, 1)

            def round_x(b):
                act.wait_ge(xT_in, 16 * (b + 1))
                nc.scalar.activation(xh[:], x1[:], ACT.Copy).then_inc(xh_ready, 1)

            mine = {s: list(v) for s, v in TAIL_PE.items()}
            mine[13] = []
            mine[14] = [("gn", 0)]
            mine[OP0 + 17] = [("ln", 0)]
            mine[OP0 + 26] = [("wt", 0)]

            def body(b, first, last):
                for s, kv, u in steps(b, first, last):
                    todo = list(preps(s, kv, last))

                    def take_prep():
                        kind, j = todo.pop(0)
                        count = prep_count(b, kv, kind, j, last)
                        if kind == "proj":
                            take_proj(j, count, b * KV + kv + 2)
                        else:
                            take_stack(j, count, kv + 1)

                    if todo and todo[0][0] == "stack":
                        take_prep()
                    exps(s, u)
                    while todo:
                        take_prep()
                    if s == NU + X_STEP and not last:
                        round_x(b + 1)
                    if lagged(b, s, LAG_T, first):
                        take_probsT(*lagged(b, s, LAG_T, first))
                    if not first:
                        for task in mine.get(s, []):
                            tail_task(b - 1, task)

            def end(b):
                for s in range(LAG_T):
                    take_probsT(*lagged(b, s, LAG_T, False))
                for s in sorted(mine):
                    for task in mine[s]:
                        tail_task(b - 1, task)

            round_x(0)
            act.wait_ge(lam_step, 3)
            nc.scalar.activation(lam_e[:], lam_s[:], ACT.Exp).then_inc(lam_exp, 1)
            for n in range(2):
                for t in range(NT):
                    take_proj(t, n * NT + t + 1, n)
            act.wait_ge(wsplit_stored, 16 * KV)
            for g in range(NG):
                take_stack(g, 2 * NT + g + 1, 0)
            batches(nc.scalar, body, end)

        @block.vector
        def _(dve):
            def high_parts(n):
                dve.wait_ge(rope_done, n + 1)
                if not (isinstance(n, int) and n == 0):
                    dve.wait_ge(prep_full, stack_read(n - 1))
                r2 = roped[:].rearrange("p t g d -> p (t g) d")
                s4 = split[:].rearrange("p (t g) f -> p t g f", g=NG)
                nc.vector.tensor_copy(split[:, :, 0:DH].bitcast(F32R), r2)
                nc.vector.tensor_copy(s4[:, :, 0:2 * RK, DH:2 * DH].bitcast(F32R), roped[:, :, 0:2 * RK, :])
                nc.vector.tensor_copy(s4[:, :, 2 * RK:NG, 2 * DH:3 * DH].bitcast(F32R),
                                      roped[:, :, 2 * RK:NG, :]).then_inc(hi_done, 1)

            def stack_read(n):
                if isinstance(n, int) and n == 0:
                    return PREP_LEAD
                return PREP_LEAD + PREP_N * (n - 1) + PREP_ORDER.index(("stack", NG - 1)) + 1

            def maxes(s, u):
                i, heads = UNITS[s % NU]
                dve.wait_ge(scores_ready, u + 1)
                slot, w, k = (256 if i < 2 else 512), P * (i + 1), 2 * len(heads)
                v = S[s % 2][:, 0:k * slot].rearrange("p (k w) -> p k w", w=slot)[:, :, 0:w]
                nc.vector.tensor_reduce(neg_max[s % 3][:, 0:k], v, AX, ALU.max, negate=True).then_inc(max_ready, 1)

            def inverse_sums(sl, u):
                i, heads = UNITS[sl % NU]
                kv = sl // NU
                h0, nh = heads[0], len(heads)
                dve.wait_ge(exp_done, u + 1)
                L, Q = sums[kv % 2], rsum[kv % 2]
                nc.vector.reciprocal(Q[:, i, :, h0:h0 + nh], L[:, i, :, h0:h0 + nh]).then_inc(rsum_step, 1)

            def ratios(sl, u):
                i, heads = UNITS[sl % NU]
                kv = sl // NU
                h0, nh = heads[0], len(heads)
                L, Q, rr = sums[kv % 2], rsum[kv % 2], rho[kv % 2]
                dve.wait_ge(rsum_step, u + 1)
                nc.vector.scalar_tensor_tensor(out=rr[:, i, h0:h0 + nh], in0=L[:, i, 0, h0:h0 + nh],
                                               scalar=neg_lam[:, 0:1], in1=Q[:, i, 1, h0:h0 + nh],
                                               op0=ALU.mult, op1=ALU.mult).then_inc(rho_step, 1)

            def mix(sl, u):
                i, heads = UNITS[sl % NU]
                rr = rho[sl // NU % 2]
                slot, w = (256 if i < 2 else 512), P * (i + 1)
                dve.wait_ge(rho_step, u + 1)
                at_least(dve, pT_full, u - 2)
                for a, h in enumerate(heads):
                    e1 = expd[sl % 3][:, 2 * a * slot:2 * a * slot + w]
                    e2 = expd[sl % 3][:, (2 * a + 1) * slot:(2 * a + 1) * slot + w]
                    ins = nc.vector.scalar_tensor_tensor(out=mixed[sl % 3][:, a * 256:a * 256 + w], in0=e2,
                                                         scalar=rr[:, i, h:h + 1], in1=e1, op0=ALU.mult, op1=ALU.add)
                ins.then_inc(mix_ready, 1)

            def scale_out(b, sl, u):
                i, heads = UNITS[sl % NU]
                kv = sl // NU
                if heads[-1] != RK - 1:
                    return
                dve.wait_ge(ctx_full, u + 1)
                if i == 0 and not (isinstance(b, int) and b == 0):
                    dve.wait_ge(tail_full, tail_count(b - 1, "ctxT", (kv + 1) * (FC // KV) - 1))
                nc.vector.tensor_tensor(ctxn[:, i, kv * RK * HD:(kv + 1) * RK * HD].rearrange("p (h d) -> p h d", h=RK),
                                        O[:], rsum[kv % 2][:, i, 0, :].unsqueeze(2).broadcast_to([P, RK, HD]),
                                        ALU.mult).then_inc(ctx_scaled, 1)

            links = [0]
            LINKS = 21

            def link(b, ins):
                links[0] += 1
                ins.then_inc(t_step, 1)
                dve.wait_ge(t_step, b * LINKS + links[0])

            def tail_work(b, what, j):
                if what == "bn":
                    dve.wait_ge(tail_act, b * len(ACT_TAIL) + j + 1)
                    ins = nc.vector.bn_stats(out=bn[:, j, :], in_=ctxT[:, j, :])
                    if j == FC - 1:
                        link(b, ins)
                        apart(dve)
                elif what == "gstats":
                    for c in range(FC):
                        ins = nc.vector.bn_aggr(st[:, c, :], bn[:, c, :])
                    link(b, ins)
                    nc.vector.tensor_copy(st2[:, :, 0], st[:, :, 0])
                    link(b, nc.vector.tensor_tensor(st2[:, :, 1], st[:, :, 0], st[:, :, 0], ALU.mult))
                    nc.vector.tensor_tensor(st2[:, :, 1], st2[:, :, 1], st[:, :, 1], ALU.add).then_inc(st_ready, 1)
                elif what == "gvar":
                    dve.wait_ge(tail_full, tail_count(b, "gn", 0))
                    ins = nc.vector.tensor_copy(gst[:].rearrange("p c s -> p (c s)"), tail[:, 0:2 * FC])
                    ins.then_inc(tail_dve, 1)
                    dve.wait_ge(tail_dve, b * len(DVE_TAIL) + 1)
                    link(b, nc.vector.tensor_tensor(gvar[:], gst[:, :, 0], gst[:, :, 0], ALU.mult))
                    nc.vector.tensor_tensor(gvar[:], gst[:, :, 1], gvar[:], ALU.subtract).then_inc(gvar_ready, 1)
                elif what == "gaffine":
                    dve.wait_ge(gsd_ready, b + 1)
                    link(b, nc.vector.reciprocal(grs[:], gsd[:]))
                    link(b, nc.vector.scalar_tensor_tensor(out=gsc[:], in0=grs[:], scalar=1.0 - LAMBDA_INIT, in1=gnw[:],
                                                           op0=ALU.mult, op1=ALU.mult))
                    link(b, nc.vector.tensor_tensor(gms[:], gst[:, :, 0], gsc[:], ALU.mult))
                    link(b, nc.vector.scalar_tensor_tensor(out=gbi[:], in0=gnb[:], scalar=1.0 - LAMBDA_INIT, in1=gms[:],
                                                           op0=ALU.mult, op1=ALU.subtract))
                elif what == "norm":
                    ins = nc.vector.tensor_scalar(ctxT[:, j, :], ctxT[:, j, :], gsc[:, j:j + 1], gbi[:, j:j + 1],
                                                  ALU.mult, ALU.add)
                    if j == FC - 1:
                        ins.then_inc(norm_ready, 1)
                elif what == "resid":
                    if j == 0:
                        dve.wait_ge(x_in, 16 * (b + 1))
                    dve.wait_ge(tail_full, tail_count(b, "oproj", j))
                    nc.vector.tensor_tensor(x1[:, j, :], tail[:], x1[:, j, :], ALU.add).then_inc(tail_dve, 1)
                    dve.wait_ge(tail_dve, b * len(DVE_TAIL) + DVE_TAIL.index(("oproj", j)) + 1)
                    link(b, nc.vector.bn_stats(out=bx[:, j, :], in_=x1[:, j, :]))
                    apart(dve)
                    ins = nc.vector.bn_aggr(mv[:, j, :], bx[:, j, :])
                    if j == NT - 1:
                        ins.then_inc(mv_ready, 1)
                elif what == "ln":
                    if j == 0:
                        dve.wait_ge(xsd_ready, b + 1)
                        link(b, nc.vector.reciprocal(xrs[:], xsd[:]))
                    nc.vector.tensor_scalar(x1[:, j, :], x1[:, j, :], mv[:, j, 0:1], xrs[:, j:j + 1],
                                            ALU.subtract, ALU.mult).then_inc(x1_ready, 1)
                elif what == "route":
                    dve.wait_ge(tail_full, tail_count(b, "logits", 0))
                    nc.vector.tensor_copy(lg[:].rearrange("p i e -> p (i e)"), tail[:, 0:NT * E]).then_inc(tail_dve, 1)
                    dve.wait_ge(tail_dve, b * len(DVE_TAIL) + DVE_TAIL.index(("logits", 0)) + 1)
                    apart(dve)
                    for i in range(NT):
                        ins = nc.vector.max(top[:, i, :], lg[:, i, :])
                    link(b, ins)
                    apart(dve)
                    for i in range(NT):
                        ins = nc.vector.max_index(topi[:, i, :], top[:, i, :], lg[:, i, :])
                    link(b, ins)
                    nc.vector.tensor_tensor(dl[:], top[:, :, 1], top[:, :, 0], ALU.subtract).then_inc(dl_ready, 1)
                    link(b, nc.vector.tensor_copy(topf[:], topi[:, :, 0:2]))
                    for k in range(TOPK):
                        ins = nc.vector.tensor_tensor(pick[:, k], small[:, 0], topf[:, :, k:k + 1].broadcast_to([P, NT, E]),
                                                      ALU.is_equal)
                    link(b, ins)
                    nc.vector.tensor_tensor(member[:], pick[:, 0], pick[:, 1], ALU.add).then_inc(member_ready, 1)
                elif what == "slots":
                    dve.wait_ge(tail_full, tail_count(b, "rank", 0))
                    nc.vector.tensor_tensor(rank[:].rearrange("p i e -> p (i e)"), tail[:, 0:NT * E],
                                            small[:, 1].rearrange("p i e -> p (i e)"), ALU.add).then_inc(tail_dve, 1)
                    dve.wait_ge(tail_dve, b * len(DVE_TAIL) + DVE_TAIL.index(("rank", 0)) + 1)
                    for k in range(TOPK):
                        nc.vector.tensor_tensor(pr[:, k], rank[:], pick[:, k], ALU.mult)
                    link(b, nc.vector.tensor_reduce(msum_t[:], member[:].rearrange("p i e -> p e i"), AX, ALU.add))
                    nc.vector.tensor_tensor(msum[:], msum[:], msum_t[:], ALU.add)
                    here = bass.ds(b * NT, NT)
                    link(b, nc.vector.tensor_reduce(slotf[:].rearrange("p k i -> p (k i)"),
                                                    pr[:].rearrange("p k i e -> p (k i) e"), AX, ALU.add))
                    nc.vector.tensor_copy(slots[:, here, :], slotf[:].rearrange("p k i -> p i k")).then_inc(slots_ready, 1)
                    dve.wait_ge(ed_ready, b + 1)
                    link(b, nc.vector.tensor_scalar(ed1[:], ed[:], 1.0, None, ALU.add))
                    link(b, nc.vector.reciprocal(wts[:, here, 0], ed1[:]))
                    nc.vector.tensor_tensor(wts[:, here, 1], ed[:], wts[:, here, 0], ALU.mult)

            mine = {c + 4: [("bn", c)] for c in range(FC)}
            mine[11] = mine.get(11, []) + [("gstats", 0)]
            mine[14] = [("gvar", 0)]
            mine[15] = [("gaffine", 0), ("norm", 0)]
            for c in range(1, FC):
                mine.setdefault(15 + c // 2 + c % 2, []).append(("norm", c))
            for i in range(NT):
                mine.setdefault(OP0 + 4 * i + 4, []).append(("resid", i))
            for i in range(NT):
                mine.setdefault(OP0 + 18 + i // 2, []).append(("ln", i))
            mine[OP0 + 25] = [("route", 0)]
            mine[OP0 + 27] = [("slots", 0)]

            def body(b, first, last):
                links[0] = 0
                for s, kv, u in steps(b, first, last):
                    if lagged(b, s, LAG_V + 1, first):
                        scale_out(b if s > LAG_V else b - 1, *lagged(b, s, LAG_V + 1, first))
                    maxes(s, u)
                    if lagged(b, s, 1, first):
                        inverse_sums(*lagged(b, s, 1, first))
                    if lagged(b, s, 2, first):
                        mix(*lagged(b, s, 2, first))
                    if lagged(b, s, 1, first):
                        ratios(*lagged(b, s, 1, first))
                    if s % NU == HI_STEP and not (last and kv >= KV - 2):
                        high_parts(b * KV + kv + 2 - HI_LAG)
                    if s % NU == HI_STEP and last and kv >= KV - 2 and kv - (KV - 2) < HI_LAG:
                        high_parts(b * KV + kv + 2 - HI_LAG)
                    if s == NU + X_STEP and not last:
                        low_x(b + 1)
                    if not first:
                        for what, j in mine.get(s, []):
                            tail_work(b - 1, what, j)

            def end(b):
                links[0] = 0
                inverse_sums(*lagged(b, 0, 1, False))
                mix(*lagged(b, 0, 2, False))
                ratios(*lagged(b, 0, 1, False))
                mix(*lagged(b, 1, 2, False))
                for s in range(LAG_V + 1):
                    scale_out(b - 1, *lagged(b, s, LAG_V + 1, False))
                for s in sorted(mine):
                    for what, j in mine[s]:
                        tail_work(b - 1, what, j)
                assert links[0] == LINKS, links[0]

            def low_x(b):
                dve.wait_ge(xh_ready, b + 1)
                nc.vector.tensor_tensor(xl[:], x1[:], xh[:].bitcast(F32), ALU.subtract).then_inc(xl_ready, 1)

            nc.vector.memset(ones[:], 1.0)
            nc.vector.memset(msum[:], 0.0)
            nc.vector.memset(eps_t[:], EPS).then_inc(lam_step, 1)
            low_x(0)
            dve.wait_ge(wraw_in, 16 * KV)
            for kv in range(KV):
                hi, lo = wparts[kv][:, :, 0, :], wparts[kv][:, :, 1, :]
                nc.vector.tensor_copy(hi, wraw[kv]).then_inc(wh_ready, 1)
                dve.wait_ge(wh_ready, kv + 1)
                nc.vector.tensor_tensor(lo, wraw[kv], hi.bitcast(F32), ALU.subtract).then_inc(wl_ready, 1)
            dve.wait_ge(consts_in, 16 * NCONST)
            lv = lam_in[:].rearrange("p (c two) d -> p c two d", two=2)
            nc.vector.tensor_tensor(lam_pr[:], lv[:, :, 0], lv[:, :, 1], ALU.mult).then_inc(lam_step, 1)
            dve.wait_ge(lam_step, 2)
            nc.vector.tensor_reduce(lam_s[:], lam_pr[:], AX, ALU.add).then_inc(lam_step, 1)
            dve.wait_ge(lam_exp, 1)
            nc.vector.scalar_tensor_tensor(out=neg_lam[:], in0=lam_e[:, 1:2], scalar=-LAMBDA_INIT, in1=lam_e[:, 0:1],
                                           op0=ALU.add, op1=ALU.subtract).then_inc(lam_ready, 1)
            dve.wait_ge(lam_ready, 1)
            high_parts(0)
            if HI_LAG == 0:
                high_parts(1)
            batches(nc.vector, body, end)


HI_STEP = 0
X_STEP = 8
HI_LAG = 1


def plan_block(nc, plan_d, load_weights, xs_dram, ones, msum, slots, out_slots, exp_tab, row_tab):
    with ExitStack() as ctx:
        def sb(name, shape, dt=F32):
            return ctx.enter_context(nc.sbuf_tensor(name, shape, dt))

        def sem(name):
            return ctx.enter_context(nc.semaphore(name))

        plan = sb("plan", [P, 2 * E + E * E + 2 * MT * E])
        zrow = sb("zrow", [P, D])
        cnt = sb("cnt", [P, E])
        padf = sb("padf", [P, E])
        padi = sb("padi", [P, E], U32)
        ni = sb("ni", [P, E], I32)
        ni2 = sb("ni2", [P, E], I32)
        nt = sb("nt", [P, E])
        gap = sb("gap", [P, E])
        sf = sb("sf", [P, N // P * TOPK])
        so = sb("so", [P, N // P * TOPK])
        hop = sb("hop", [P, E - 1, N // P * TOPK])
        cp = sb("cp", [1, E, E])
        ci = sb("ci", [1, E])
        ge = sb("ge", [1, MT, E])
        gn = sb("gn", [1, MT, E])
        ek = sb("ek", [1, MT])
        sk = sb("sk", [1, MT])
        live = sb("live", [1, MT])
        jk = sb("jk", [1, MT])
        rk = sb("rk", [1, MT])
        cps = ctx.enter_context(nc.psum_tensor("cps", [P, E], F32))
        plan_in = sem("plan_in")
        cnt_full = sem("cnt_full")
        chain = sem("chain")
        pad_ready = sem("pad_ready")
        padded = sem("padded")
        block = ctx.enter_context(nc.Block())
        region = plan[:, 0:E]
        incl = plan[0:1, 2 * E:2 * E + E * E].rearrange("p (a b) -> p a b", a=E)
        kio = plan[0:1, 2 * E + E * E:2 * E + E * E + MT * E].rearrange("p (k e) -> p k e", e=E)

        @block.sync
        def _(sp):
            sp.dma_start(plan[:], plan_d).then_inc(plan_in, 16)
            load_weights(sp, 0)

        @block.tensor
        def _(pe):
            nc.tensor.matmul(cps[:], ones[:], msum[:], start=True, stop=True).then_inc(cnt_full, 1)

        @block.gpsimd
        def _(pool):
            pool.wait_ge(pad_ready, 1)
            for e in range(E):
                nc.gpsimd.indirect_dma_start(xs_dram, bass.IndirectOffsetOnAxis(ap=padi[:, e:e + 1], axis=0),
                                             zrow[:], None).then_inc(padded, 16)
            pool.wait_ge(padded, 16 * E)

        @block.vector
        def _(dve):
            links = [0]

            def link(ins):
                links[0] += 1
                ins.then_inc(chain, 1)
                dve.wait_ge(chain, links[0])

            nc.vector.memset(zrow[:], 0.0)
            dve.wait_ge(plan_in, 16)
            dve.wait_ge(cnt_full, 1)
            link(nc.vector.tensor_copy(cnt[:], cps[:]))
            link(nc.vector.tensor_tensor(padf[:], cnt[:], region, ALU.add))
            nc.vector.tensor_copy(padi[:], padf[:]).then_inc(pad_ready, 1)
            link(nc.vector.tensor_scalar(nt[:], cnt[:], float(P - 1), None, ALU.add))
            link(nc.vector.tensor_copy(ni[:], nt[:]))
            link(nc.vector.tensor_scalar(ni2[:], ni[:], P.bit_length() - 1, None, ALU.arith_shift_right))
            link(nc.vector.tensor_copy(nt[:], ni2[:]))
            nc.vector.tensor_copy(sf[:], slots[:].rearrange("p t k -> p (t k)"))
            link(nc.vector.tensor_scalar(gap[:], nt[:], float(P), -float(R), ALU.mult, ALU.add))
            for e in range(1, E):
                ins = nc.vector.tensor_scalar(hop[:, e - 1, :], sf[:], float(e * R), gap[:, e - 1:e], ALU.is_ge, ALU.mult)
            link(ins)
            link(nc.vector.tensor_reduce(so[:], hop[:].rearrange("p e s -> p s e"), AX, ALU.add))
            link(nc.vector.tensor_tensor(so[:], so[:], sf[:], ALU.add))
            nc.vector.tensor_copy(out_slots[:].rearrange("p t k -> p (t k)"), so[:])
            link(nc.vector.tensor_tensor(cp[:], incl, nt[0:1, :].unsqueeze(1).broadcast_to([1, E, E]), ALU.mult))
            link(nc.vector.tensor_reduce(ci[:], cp[:], AX, ALU.add))
            link(nc.vector.tensor_tensor(ge[:], kio, ci[:].unsqueeze(1).broadcast_to([1, MT, E]), ALU.is_ge))
            link(nc.vector.tensor_tensor(gn[:], ge[:], nt[0:1, :].unsqueeze(1).broadcast_to([1, MT, E]), ALU.mult))
            nc.vector.tensor_reduce(ek[:], ge[:], AX, ALU.add)
            link(nc.vector.tensor_reduce(sk[:], gn[:], AX, ALU.add))
            link(nc.vector.tensor_scalar(live[:], ge[:, :, E - 1], -1.0, 1.0, ALU.mult, ALU.add))
            link(nc.vector.tensor_tensor(jk[:], kio[:, :, 0], sk[:], ALU.subtract))
            link(nc.vector.tensor_tensor(jk[:], jk[:], live[:], ALU.mult))
            link(nc.vector.tensor_tensor(ek[:], ek[:], live[:], ALU.mult))
            link(nc.vector.tensor_scalar(rk[:], ek[:], float(R), None, ALU.mult))
            link(nc.vector.scalar_tensor_tensor(out=rk[:], in0=jk[:], scalar=float(P), in1=rk[:],
                                                op0=ALU.mult, op1=ALU.add))
            nc.vector.tensor_copy(exp_tab[:], ek[:])
            link(nc.vector.tensor_copy(row_tab[:], rk[:]))


def expert_block(nc, wgu, wd, ew_in, load_weights, xs_dram, ys_dram, x1_dram, x_early, x_early_in, ident, exp_tab, row_tab):
    with ExitStack() as ctx:
        def sb(name, shape, dt=F32):
            return ctx.enter_context(nc.sbuf_tensor(name, shape, dt))

        def pb(name, shape):
            return ctx.enter_context(nc.psum_tensor(name, shape, F32))

        def sem(name):
            return ctx.enter_context(nc.semaphore(name))

        GU = 2 * I
        xin = [sb(f"xin{r}", [P, D]) for r in range(2)]
        xinT = [sb(f"xinT{r}", [P, D]) for r in range(2)]
        sg = [sb(f"sg{r}", [P, I]) for r in range(2)]
        hid = [sb(f"hid{r}", [P, I]) for r in range(2)]
        hidT = [sb(f"hidT{r}", [P, 3 * P]) for r in range(2)]
        yo = [sb(f"yo{r}", [P, D]) for r in range(2)]
        xTp = pb("xTp", [P, 512])
        G = [pb(f"G{r}", [P, 512]) for r in range(2)]
        U = [pb(f"U{r}", [P, 512]) for r in range(2)]
        hTp = pb("hTp", [P, 512])
        Y = [pb(f"Y{r}", [P, 512]) for r in range(2)]

        w_ready = sem("w_ready")
        rows_in = [sem(f"rows_in{r}") for r in range(2)]
        xT_full = sem("e_xT_full")
        xT_out = sem("e_xT_out")
        g_full = sem("g_full")
        gu_full = sem("gu_full")
        silu_done = sem("silu_done")
        hid_ready = sem("hid_ready")
        hT_full = sem("hT_full")
        hT_out = sem("hT_out")
        y_full = sem("y_full")
        y_out = sem("y_out")
        y_stored = [sem(f"y_stored{r}") for r in range(2)]
        block = ctx.enter_context(nc.Block())
        @block.sync
        def _(sp):
            def load(k, r, wait):
                row = nc.sync.value_load(row_tab[0:1, bass.ds(k, 1)], min_val=0, max_val=(E - 1) * R + N)
                if wait:
                    sp.wait_ge(xT_full, k - 1)
                sp.dma_start(xin[r][:], xs_dram[bass.ds(row, P), :]).then_inc(rows_in[r], 16)

            load(0, 0, False)
            load(1, 1, False)
            load_weights(sp, 1)
            for m in range(1, E - 1):
                for r in range(2):
                    load(m * 2 + r, r, True)
                load_weights(sp, m + 1)
            with nc.sync.Fori(E - 1, E - 1 + EARLY) as m:
                for r in range(2):
                    load(m * 2 + r, r, True)
                t = m - (E - 1)
                sp.dma_start(x_early[:, bass.ds(t, 1), :].rearrange("p a d -> p (a d)"),
                             x1_dram[bass.ds(t * P, P), :]).then_inc(x_early_in, 16)
            with nc.sync.Fori(E - 1 + EARLY, MT // 2) as m:
                for r in range(2):
                    load(m * 2 + r, r, True)

        @block.scalar
        def _(act):
            def take_xT(k, r):
                act.wait_ge(xT_full, k + 1)
                if not (isinstance(k, int) and k < 2):
                    act.wait_ge(gu_full, k - 1)
                nc.scalar.activation(xinT[r][:], xTp[:], ACT.Copy).then_inc(xT_out, 1)

            def silu(k, r):
                act.wait_ge(g_full, k + 1)
                if not (isinstance(k, int) and k < 2):
                    act.wait_ge(hid_ready, k - 1)
                nc.scalar.activation(sg[r][:], G[r][:, 0:I], ACT.Silu).then_inc(silu_done, 1)

            def store(k, r):
                act.wait_ge(y_out, k + 1)
                act.dma_start(ys_dram[bass.ds(k * P, P), :], yo[r][:]).then_inc(y_stored[r], 16)

            take_xT(0, 0)
            take_xT(1, 1)
            silu(0, 0)

            def pair(m):
                for r in range(2):
                    k = m * 2 + r
                    take_xT(k + 2, r)
                    silu(k + 1, 1 - r)
                    store(k, r)

            pair(0)
            with nc.scalar.Fori(1, MT // 2 - 1) as m:
                pair(m)
            silu(MT - 1, 1)
            store(MT - 2, 0)
            store(MT - 1, 1)
            for r in range(2):
                act.wait_ge(y_stored[r], 16 * MT // 2)

        @block.gpsimd
        def _(pool):
            for e in range(E):
                pool.wait_ge(ew_in[e], 16 * 4)
                pool.sem_inc(w_ready, 1)

        @block.tensor
        def _(pe):
            def expert(k):
                return nc.tensor.value_load(exp_tab[0:1, bass.ds(k, 1)], min_val=0, max_val=E - 1)

            def x_transpose(k, r):
                pe.wait_ge(rows_in[r], fills(k, r))
                if not (isinstance(k, int) and k == 0):
                    pe.wait_ge(xT_out, k)
                for c in range(DC):
                    mm = nc.tensor.transpose(xTp[:, c * P:(c + 1) * P], xin[r][:, c * P:(c + 1) * P], ident[:])
                mm.then_inc(xT_full, 1)

            def fills(k, r):
                return 16 * (k // 2 + 1) if isinstance(k, int) else (k - r) * 8 + 16

            def gate_up(k, r, half, e):
                if half == 0:
                    pe.wait_ge(w_ready, e + 1)
                    pe.wait_ge(xT_out, k + 1)
                    if not (isinstance(k, int) and k < 2):
                        pe.wait_ge(hid_ready, k - 1)
                ps = (G, U)[half][r]
                for c in range(DC):
                    mm = nc.tensor.matmul(ps[:, 0:I], xinT[r][:, c * P:(c + 1) * P],
                                          wgu[:, bass.ds(e * (DC * GU) + (c * GU + half * I), I)],
                                          start=(c == 0), stop=(c == DC - 1))
                mm.then_inc((g_full, gu_full)[half], 1)

            def h_transpose(k, r):
                pe.wait_ge(hid_ready, k + 1)
                if not (isinstance(k, int) and k == 0):
                    pe.wait_ge(hT_out, k)
                for n, (o, w) in enumerate(IC):
                    mm = nc.tensor.transpose(hTp[0:w, n * P:(n + 1) * P], hid[r][:, o:o + w], ident[:])
                mm.then_inc(hT_full, 1)

            def down(k, r, e):
                pe.wait_ge(hT_out, k + 1)
                if not (isinstance(k, int) and k < 2):
                    pe.wait_ge(y_out, k - 1)
                for n, (o, w) in enumerate(IC):
                    mm = nc.tensor.matmul(Y[r][:], hidT[r][0:w, n * P:(n + 1) * P],
                                          wd[0:w, bass.ds(e * (len(IC) * D) + n * D, D)],
                                          start=(n == 0), stop=(n == len(IC) - 1))
                mm.then_inc(y_full, 1)

            def step(k, r, last=False):
                if not last:
                    e1 = expert(k + 1)
                    gate_up(k + 1, 1 - r, 0, e1)
                h_transpose(k, r)
                if not last:
                    gate_up(k + 1, 1 - r, 1, e1)
                down(k, r, expert(k))

            x_transpose(0, 0)
            x_transpose(1, 1)
            e0 = expert(0)
            gate_up(0, 0, 0, e0)
            gate_up(0, 0, 1, e0)

            def pair(m):
                for r in range(2):
                    k = m * 2 + r
                    x_transpose(k + 2, r)
                    step(k, r)

            pair(0)
            with nc.tensor.Fori(1, MT // 2 - 1) as m:
                pair(m)
            step(MT - 2, 0)
            step(MT - 1, 1, last=True)

        @block.vector
        def _(dve):
            def hidden(k, r):
                dve.wait_ge(silu_done, k + 1)
                dve.wait_ge(gu_full, k + 1)
                if not (isinstance(k, int) and k < 2):
                    dve.wait_ge(hT_full, k - 1)
                nc.vector.tensor_tensor(hid[r][:], U[r][:, 0:I], sg[r][:], ALU.mult).then_inc(hid_ready, 1)

            def take_hT(k, r):
                dve.wait_ge(hT_full, k + 1)
                if not (isinstance(k, int) and k < 2):
                    dve.wait_ge(y_full, k - 1)
                nc.vector.tensor_copy(hidT[r][:, 0:2 * P], hTp[:, 0:2 * P])
                w = I - 2 * P
                nc.vector.tensor_copy(hidT[r][0:w, 2 * P:3 * P], hTp[0:w, 2 * P:3 * P]).then_inc(hT_out, 1)

            def take_y(k, r):
                dve.wait_ge(y_full, k + 1)
                if not (isinstance(k, int) and k < 2):
                    dve.wait_ge(y_stored[r], 16 * (k // 2) if isinstance(k, int) else (k - r) * 8)
                nc.vector.tensor_copy(yo[r][:], Y[r][:]).then_inc(y_out, 1)

            hidden(0, 0)
            take_hT(0, 0)

            def pair(m):
                for r in range(2):
                    k = m * 2 + r
                    hidden(k + 1, 1 - r)
                    take_y(k, r)
                    take_hT(k + 1, 1 - r)

            pair(0)
            with nc.vector.Fori(1, MT // 2 - 1) as m:
                pair(m)
            hidden(MT - 1, 1)
            take_y(MT - 2, 0)
            take_hT(MT - 1, 1)
            take_y(MT - 1, 1)


def combine_block(nc, x1_dram, ys_dram, slots, wts, x_early, x_early_in, out):
    NTT = N // P
    with ExitStack() as ctx:
        def sb(name, shape, dt=F32):
            return ctx.enter_context(nc.sbuf_tensor(name, shape, dt))

        def sem(name):
            return ctx.enter_context(nc.semaphore(name))

        G = EARLY
        ya = [sb(f"ya{r}", [P, TOPK, D]) for r in range(G)]
        x_late = sb("x_late", [P, NTT - G, D])
        res = [sb(f"res{r}", [P, D]) for r in range(G)]
        idx = [sb(f"cidx{r}", [P, TOPK], U32) for r in range(G)]
        bs = [sb(f"bs{r}", [P, 6]) for r in range(G)]
        mv = [sb(f"cmv{r}", [P, 2]) for r in range(G)]
        sd = [sb(f"sd{r}", [P, 1]) for r in range(G)]
        rs = [sb(f"rs{r}", [P, 1]) for r in range(G)]
        nb = [sb(f"nb{r}", [P, 1]) for r in range(G)]
        eps_t = sb("ceps", [P, 1])
        gathered = [sem(f"gathered{r}") for r in range(G)]
        x_in = [sem(f"cx_in{r}") for r in range(G)]
        idx_ready = sem("cidx_ready")
        first_added = sem("first_added")
        summed = sem("summed")
        bn_done = sem("bn_done")
        mv_ready = sem("cmv_ready")
        sd_ready = sem("sd_ready")
        rs_ready = sem("rs_ready")
        nb_ready = sem("nb_ready")
        eps_set = sem("eps_set")
        done = sem("cdone")
        stored = [sem(f"stored{r}") for r in range(G)]
        waited = sem("cwaited")

        def apart(e):
            e.sem_inc(waited, 1)

        block = ctx.enter_context(nc.Block())
        rounds = NTT // G
        out_f = out.rearrange("b t d -> (b t) d")

        @block.sync
        def _(sp):
            with nc.sync.Fori(1, rounds) as m:
                for r in range(G):
                    t = m * G + r
                    sp.wait_ge(idx_ready, t + 1)
                    sp.dma_start(x_late[:, bass.ds(t - G, 1), :].rearrange("p a d -> p (a d)"),
                                 x1_dram[bass.ds(t * P, P), :]).then_inc(x_in[r], 16)

        @block.gpsimd
        def _(pool):
            def gather(t, r, wait):
                if wait:
                    pool.wait_ge(summed, t - G + 1)
                    apart(pool)
                nc.gpsimd.tensor_copy(idx[r][:], slots[:, bass.ds(t, 1), :].rearrange("p a k -> p (a k)")) \
                  .then_inc(idx_ready, 1)
                pool.wait_ge(idx_ready, t + 1)
                apart(pool)
                for k in range(TOPK):
                    nc.gpsimd.indirect_dma_start(ya[r][:, k, :], None, ys_dram,
                                                 bass.IndirectOffsetOnAxis(ap=idx[r][:, k:k + 1], axis=0)) \
                      .then_inc(gathered[r], 16)

            for r in range(G):
                gather(r, r, False)
            with nc.gpsimd.Fori(1, rounds) as m:
                for r in range(G):
                    gather(m * G + r, r, True)

        @block.scalar
        def _(act):
            def root(t, r):
                act.wait_ge(mv_ready, t + 1)
                nc.scalar.activation(sd[r][:], mv[r][:, 1:2], ACT.Sqrt, bias=eps_t[:, 0:1]).then_inc(sd_ready, 1)

            def normalise(t, r):
                act.wait_ge(nb_ready, t + 1)
                nc.scalar.activation(res[r][:], res[r][:], ACT.Identity, bias=nb[r][:, 0:1],
                                     scale=rs[r][:, 0:1]).then_inc(done, 1)
                act.wait_ge(done, t + 1)
                act.dma_start(out_f[bass.ds(t * P, P), :], res[r][:]).then_inc(stored[r], 16)

            act.wait_ge(eps_set, 1)
            for r in range(G):
                root(r, r)
                if r >= 1:
                    normalise(r - 1, r - 1)
            with nc.scalar.Fori(1, rounds) as m:
                for r in range(G):
                    t = m * G + r
                    root(t, r)
                    normalise(t - 1, (r - 1) % G)
            normalise(NTT - 1, G - 1)
            for r in range(G):
                act.wait_ge(stored[r], 16 * rounds)

        @block.vector
        def _(dve):
            nc.vector.memset(eps_t[:], EPS).then_inc(eps_set, 1)

            def weights(t):
                return wts[:, bass.ds(t, 1), :].rearrange("p a k -> p (a k)")

            def add_first(m, r):
                t = m * G + r
                dve.wait_ge(gathered[r], 32 * (m + 1))
                if isinstance(m, int):
                    xr = x_early[:, r, :]
                else:
                    xr = x_late[:, bass.ds(t - G, 1), :].rearrange("p a d -> p (a d)")
                    dve.wait_ge(x_in[r], 16 * m)
                    dve.wait_ge(stored[r], 16 * m)
                nc.vector.scalar_tensor_tensor(out=res[r][:], in0=ya[r][:, 0, :], scalar=weights(t)[:, 0:1], in1=xr,
                                               op0=ALU.mult, op1=ALU.add).then_inc(first_added, 1)

            def add_second(t, r):
                dve.wait_ge(first_added, t + 1)
                nc.vector.scalar_tensor_tensor(out=res[r][:], in0=ya[r][:, 1, :], scalar=weights(t)[:, 1:2],
                                               in1=res[r][:], op0=ALU.mult, op1=ALU.add).then_inc(summed, 1)

            def stats(t, r):
                dve.wait_ge(summed, t + 1)
                nc.vector.bn_stats(out=bs[r][:], in_=res[r][:]).then_inc(bn_done, 1)

            def moments(t, r):
                dve.wait_ge(bn_done, t + 1)
                apart(dve)
                nc.vector.bn_aggr(mv[r][:], bs[r][:]).then_inc(mv_ready, 1)

            def inverse(t, r):
                dve.wait_ge(sd_ready, t + 1)
                nc.vector.reciprocal(rs[r][:], sd[r][:]).then_inc(rs_ready, 1)

            def offset(t, r):
                dve.wait_ge(rs_ready, t + 1)
                nc.vector.scalar_tensor_tensor(out=nb[r][:], in0=mv[r][:, 0:1], scalar=-1.0, in1=rs[r][:],
                                               op0=ALU.mult, op1=ALU.mult).then_inc(nb_ready, 1)

            def step(m, r):
                t = m * G + r
                one, two = not isinstance(m, int) or r >= 1, not isinstance(m, int) or r >= 2
                add_first(m, r)
                if one:
                    moments(t - 1, (r - 1) % G)
                add_second(t, r)
                if two:
                    inverse(t - 2, (r - 2) % G)
                stats(t, r)
                if two:
                    offset(t - 2, (r - 2) % G)

            dve.wait_ge(x_early_in, 16 * EARLY)
            for r in range(G):
                step(0, r)
            with nc.vector.Fori(1, rounds) as m:
                for r in range(G):
                    step(m, r)
            moments(NTT - 1, G - 1)
            for t in (NTT - 2, NTT - 1):
                inverse(t, t % G)
                offset(t, t % G)


def kernel(L0_attn_x, L0_attn_Wq, L0_attn_Wk, L0_attn_Wv, L0_attn_Wo, L0_attn_lambda_q1, L0_attn_lambda_k1,
           L0_attn_lambda_q2, L0_attn_lambda_k2, L0_attn_gn_w, L0_attn_gn_b, L0_ffn_gate_w, L0_ffn_w_gate,
           L0_ffn_w_up, L0_ffn_w_down):
    import concourse.bacc as _bacc
    from concourse.bass_utils import run_bass_kernel_spmd as _run
    import ml_dtypes

    def c(a):
        return np.ascontiguousarray(np.asarray(a))

    x = c(L0_attn_x)
    Wq, Wk, Wv = (c(a).reshape(DC, P, KV, -1) for a in (L0_attn_Wq, L0_attn_Wk, L0_attn_Wv))
    arrays = {
        "x": x,
        "xT": c(x.reshape(B, T, DC, P).transpose(3, 0, 2, 1)),
        "wqkv": c(np.concatenate([Wq, Wk, Wv], axis=3).transpose(1, 0, 2, 3)),
        "wo": c(c(L0_attn_Wo).reshape(FC, P, D).transpose(1, 0, 2)),
        "lam": c(np.stack([c(L0_attn_lambda_q1), c(L0_attn_lambda_k1), c(L0_attn_lambda_q2), c(L0_attn_lambda_k2)])),
        "gnw": c(c(L0_attn_gn_w).reshape(FC, P).T),
        "gnb": c(c(L0_attn_gn_b).reshape(FC, P).T),
        "gate": c(c(L0_ffn_gate_w).T.reshape(DC, P, E).transpose(1, 0, 2)),
        "wg": c(L0_ffn_w_gate),
        "wu": c(L0_ffn_w_up),
        "wd": c(L0_ffn_w_down),
    }
    inv = (np.float32(1.0) / np.power(np.float32(10000.0), np.arange(0, DH, 2, dtype=np.float32) / np.float32(DH))).astype(np.float32)
    fr = (np.arange(T, dtype=np.float32)[:, None] * inv[None, :]).astype(np.float32)
    for name, f in (("rope_cos", np.cos), ("rope_sin", np.sin)):
        t = f(fr.astype(np.float64)).reshape(NT, P, 1, DH // 2).transpose(1, 0, 2, 3)
        arrays[name] = c(np.concatenate([t / math.sqrt(DH), t], axis=2).astype(np.float32))
    eye = np.eye(P, dtype=np.float32)
    arrays["ident"] = eye
    arrays["identb"] = eye.astype(ml_dtypes.bfloat16)
    arrays["maskb"] = np.where(np.arange(P)[None, :] > np.arange(P)[:, None], NEG, 0.0).astype(ml_dtypes.bfloat16)
    arrays["tri"] = (np.arange(P)[:, None] < np.arange(P)[None, :]).astype(np.float32)
    same = np.arange(P)[:, None] // HD == np.arange(P)[None, :] // HD
    arrays["avg"] = (same / HD).astype(np.float32)
    en = np.arange(E, dtype=np.float32)
    arrays["small"] = c(np.broadcast_to(np.stack([en, en * R])[None, :, None, :], (P, 2, NT, E)))
    region = en[None, :] * R + np.arange(P, dtype=np.float32)[:, None]
    incl = (np.arange(E)[None, :] <= np.arange(E)[:, None]).astype(np.float32).reshape(1, -1)
    kio = np.repeat(np.arange(MT, dtype=np.float32), E).reshape(1, -1)
    rest = np.concatenate([np.zeros((1, E), np.float32), incl, kio, kio], axis=1)
    arrays["plan"] = c(np.concatenate([region, np.broadcast_to(rest, (P, rest.shape[1]))], axis=1).astype(np.float32))

    nc = _bacc.Bacc("TRN2", target_bir_lowering=False, num_devices=1)
    names = ["x", "xT", "wqkv", "wo", "lam", "gnw", "gnb", "gate", "wg", "wu", "wd", "rope_cos", "rope_sin",
             "ident", "identb", "maskb", "tri", "avg", "small", "plan"]
    args = [nc.dram_tensor(f"in_{n}", arrays[n].shape, mybir.dt.from_np(arrays[n].dtype), kind="ExternalInput").ap()
            for n in names]
    o = nc.dram_tensor("out_y", (B, T, D), F32, kind="ExternalOutput").ap()
    layer_kernel(nc, *args, o)
    r = _run(nc, [{f"in_{n}": arrays[n] for n in names}], core_ids=[0])
    return r.results[0]["out_y"]
```
